# Optimizing a Trainium2 kernel written in Bass

```python
import numpy as np
import jax
import jax.numpy as jnp

def _softmax(x, axis=-1):
    return jax.nn.softmax(x, axis=axis)

def _gelu(x):
    return jax.nn.gelu(x, approximate=True)

def _silu(x):
    return jax.nn.silu(x)

def _sigmoid(x):
    return jax.nn.sigmoid(x)

def _layernorm(x, axis=-1, eps=1e-05):
    m = jnp.mean(x, axis=axis, keepdims=True)
    v = jnp.var(x, axis=axis, keepdims=True)
    return (x - m) / jnp.sqrt(v + eps)

def _scatter_add(tgt, idx, src, axis=0):
    return tgt.at[idx].add(src)

def _segment_sum(src, seg, n):
    return jax.ops.segment_sum(src, seg, n)
kernel_name = 'mk_adj_resnorm_d2_adj_r2_09e47f'

def setup_inputs(seed: int=0):
    np.random.seed(seed)
    _w = jnp.asarray

    def _rec_inputs():
        import jax
        import jax.numpy as jnp
        _gk = jax.random.key(seed)
        x = 0.5001 + 0.2887 * jax.random.normal(jax.random.fold_in(_gk, 1), (8192, 64), jnp.float32)
        _a = jax.random.bernoulli(jax.random.fold_in(_gk, 2), 0.000488281, (8192, 8192))
        _a = jnp.logical_or(_a, jnp.swapaxes(_a, -1, -2))
        _a = jnp.logical_or(_a, jnp.eye(8192, dtype=bool))
        _af = _a.astype(jnp.float32)
        _af = _af * jax.random.uniform(jax.random.fold_in(_gk, 3), (8192, 8192), jnp.float32, 0.05, 1)
        adj = _af
        return (x, adj)
    x, adj = _rec_inputs()

    def _L0_gnn_setup():
        import jax, jax.numpy as jnp
        import numpy as np
        N = 5000
        DIM = 64
        F_CONST = 1.0
        B_CONST = 0.1
        R_CONST = 0.01
        key = jax.random.key(seed)
        k1, k2 = jax.random.split(key)
        t = jnp.zeros((1,), dtype=jnp.float32)
        x = jax.random.uniform(k1, (N, DIM), dtype=jnp.float32)
        A = jax.random.uniform(k2, (N, N), dtype=jnp.float32)
        return {'t': t, 'x': x, 'A': A}
    _L0_gnn_all = _L0_gnn_setup()
    _L0_gnn_in = {k: v for k, v in _L0_gnn_all.items() if k in ('t',)}
    del _L0_gnn_all

    def _L1_gnn_setup():
        import jax, jax.numpy as jnp
        import numpy as np
        N = 4096
        H = 64
        ALPHA = 0.2
        NEG_INF = -9000000000000000.0

        def gru_cell(x, h, w_ih, w_hh, b_ih, b_hh):
            gi = x @ w_ih.T + b_ih
            gh = h @ w_hh.T + b_hh
            ir, iz, inn = jnp.split(gi, 3, axis=1)
            hr, hz, hn = jnp.split(gh, 3, axis=1)
            r = jax.nn.sigmoid(ir + hr)
            z = jax.nn.sigmoid(iz + hz)
            n = jnp.tanh(inn + r * hn)
            return (1.0 - z) * n + z * h

        def gat(h, node_adj, edge_adj, W, a):
            hw = h @ W
            h_plus = (node_adj > 0).astype(hw.dtype) @ hw
            h_minus = (node_adj < 0).astype(hw.dtype) @ hw
            e_plus = jax.nn.leaky_relu(jnp.concatenate([h_plus, h_minus], axis=1) @ a, ALPHA)
            e_minus = jax.nn.leaky_relu(jnp.concatenate([h_minus, h_plus], axis=1) @ a, ALPHA)
            att = jnp.where(edge_adj > 0, e_plus, NEG_INF)
            att = jnp.where(edge_adj < 0, e_minus, att)
            att = jax.nn.softmax(att, axis=1)
            return att * edge_adj @ hw
        key = jax.random.key(seed)
        ks = jax.random.split(key, 12)
        f32 = jnp.float32
        inp = {'h': jax.random.normal(ks[0], (N, H), f32), 'node_adj': jax.random.normal(ks[1], (N, N), f32), 'edge_adj': jax.random.normal(ks[2], (N, N), f32), 'W_gat': jax.random.normal(ks[3], (H, H), f32) * (1.414 * np.sqrt(6.0 / (2 * H))), 'a_gat': jax.random.normal(ks[4], (2 * H, 1), f32) * (1.414 * np.sqrt(6.0 / (2 * H + 1))), 'w_ih_e': jax.random.normal(ks[5], (3 * H, 2 * H), f32) * 0.01, 'w_hh_e': jax.random.normal(ks[6], (3 * H, H), f32) * 0.01, 'b_ih_e': jnp.zeros((3 * H,), f32), 'b_hh_e': jnp.zeros((3 * H,), f32), 'w_ih_n': jax.random.normal(ks[7], (3 * H, H), f32) * 0.01, 'w_hh_n': jax.random.normal(ks[8], (3 * H, H), f32) * 0.01, 'b_ih_n': jnp.zeros((3 * H,), f32), 'b_hh_n': jnp.zeros((3 * H,), f32)}
        return inp
    _L1_gnn_all = _L1_gnn_setup()
    _L1_gnn_in = {k: v for k, v in _L1_gnn_all.items() if k in ('W_gat', 'a_gat', 'w_ih_e', 'w_hh_e', 'b_ih_e', 'b_hh_e', 'w_ih_n', 'w_hh_n', 'b_ih_n', 'b_hh_n')}
    del _L1_gnn_all
    return {'x': x, 'adj': adj, 'L0_gnn_t': _L0_gnn_in['t'], 'L1_gnn_W_gat': _L1_gnn_in['W_gat'], 'L1_gnn_a_gat': _L1_gnn_in['a_gat'], 'L1_gnn_w_ih_e': _L1_gnn_in['w_ih_e'], 'L1_gnn_w_hh_e': _L1_gnn_in['w_hh_e'], 'L1_gnn_b_ih_e': _L1_gnn_in['b_ih_e'], 'L1_gnn_b_hh_e': _L1_gnn_in['b_hh_e'], 'L1_gnn_w_ih_n': _L1_gnn_in['w_ih_n'], 'L1_gnn_w_hh_n': _L1_gnn_in['w_hh_n'], 'L1_gnn_b_ih_n': _L1_gnn_in['b_ih_n'], 'L1_gnn_b_hh_n': _L1_gnn_in['b_hh_n']}

def reference(x, adj, L0_gnn_t, L1_gnn_W_gat, L1_gnn_a_gat, L1_gnn_w_ih_e, L1_gnn_w_hh_e, L1_gnn_b_ih_e, L1_gnn_b_hh_e, L1_gnn_w_ih_n, L1_gnn_w_hh_n, L1_gnn_b_ih_n, L1_gnn_b_hh_n):
    import jax
    import jax.numpy as jnp

    def _L0_gnn_ref(t, x, A):
        import jax, jax.numpy as jnp
        import numpy as np
        N = 5000
        DIM = 64
        F_CONST = 1.0
        B_CONST = 0.1
        R_CONST = 0.01
        Ax = A @ x
        outer = R_CONST * jnp.sum(x * Ax, axis=1, keepdims=True)
        return F_CONST - B_CONST * x - outer

    def _L1_gnn_ref(h, node_adj, edge_adj, W_gat, a_gat, w_ih_e, w_hh_e, b_ih_e, b_hh_e, w_ih_n, w_hh_n, b_ih_n, b_hh_n):
        import jax, jax.numpy as jnp
        import numpy as np
        N = 4096
        H = 64
        ALPHA = 0.2
        NEG_INF = -9000000000000000.0

        def gru_cell(x, h, w_ih, w_hh, b_ih, b_hh):
            gi = x @ w_ih.T + b_ih
            gh = h @ w_hh.T + b_hh
            ir, iz, inn = jnp.split(gi, 3, axis=1)
            hr, hz, hn = jnp.split(gh, 3, axis=1)
            r = jax.nn.sigmoid(ir + hr)
            z = jax.nn.sigmoid(iz + hz)
            n = jnp.tanh(inn + r * hn)
            return (1.0 - z) * n + z * h

        def gat(h, node_adj, edge_adj, W, a):
            hw = h @ W
            h_plus = (node_adj > 0).astype(hw.dtype) @ hw
            h_minus = (node_adj < 0).astype(hw.dtype) @ hw
            e_plus = jax.nn.leaky_relu(jnp.concatenate([h_plus, h_minus], axis=1) @ a, ALPHA)
            e_minus = jax.nn.leaky_relu(jnp.concatenate([h_minus, h_plus], axis=1) @ a, ALPHA)
            att = jnp.where(edge_adj > 0, e_plus, NEG_INF)
            att = jnp.where(edge_adj < 0, e_minus, att)
            att = jax.nn.softmax(att, axis=1)
            return att * edge_adj @ hw
        d_node = jnp.diag(node_adj)
        d_edge = jnp.diag(edge_adj)
        A_node = node_adj - jnp.diag(d_node)
        A_edge = edge_adj - jnp.diag(d_edge)
        node_support = jnp.concatenate([(A_node > 0).astype(h.dtype) @ h, (A_node < 0).astype(h.dtype) @ h], axis=1)
        edge_output = gru_cell(node_support, h, w_ih_e, w_hh_e, b_ih_e, b_hh_e)
        edge_support = gat(h, A_node, A_edge, W_gat, a_gat)
        node_output = gru_cell(edge_support, h, w_ih_n, w_hh_n, b_ih_n, b_hh_n)
        return d_edge[:, None] * edge_output + d_node[:, None] * node_output
    x = _layernorm(x + _L0_gnn_ref(L0_gnn_t, x, adj), axis=-1)
    x = _layernorm(x + _L1_gnn_ref(x, adj, adj, L1_gnn_W_gat, L1_gnn_a_gat, L1_gnn_w_ih_e, L1_gnn_w_hh_e, L1_gnn_b_ih_e, L1_gnn_b_hh_e, L1_gnn_w_ih_n, L1_gnn_w_hh_n, L1_gnn_b_ih_n, L1_gnn_b_hh_n), axis=-1)
    return x

_drawn_inputs = setup_inputs


def setup_inputs(seed=0):
    import zlib

    import numpy as np

    out = dict(_drawn_inputs(seed))
    spreads = {'L1_gnn_b_ih_e': (0.0, 0.36),
     'L1_gnn_b_hh_e': (0.0, 0.701),
     'L1_gnn_b_ih_n': (0.0, 0.4),
     'L1_gnn_b_hh_n': (0.0, 0.697)}
    factors = {'L1_gnn_W_gat': 6.741,
     'L1_gnn_w_hh_e': 6.071,
     'L1_gnn_w_ih_n': 6.818,
     'L1_gnn_w_hh_n': 6.075}
    for name, (base, spread) in spreads.items():
        noise = np.random.default_rng([zlib.crc32(name.encode()), seed]).standard_normal(out[name].shape)
        drawn = base * np.exp(spread * noise) if base else spread * noise
        out[name] = jnp.asarray(drawn.astype(out[name].dtype))
    for name, factor in factors.items():
        out[name] = (out[name] * factor).astype(out[name].dtype)
    return out
```

```python
from contextlib import ExitStack

import concourse.bass as bass
from concourse import mybir

P = 128
Q = 32
G = P // Q
BANK = 512
D = 64
EPS = 1e-5
ALPHA = 0.2
NEG_INF = -9000000000000000.0
F_CONST, B_CONST, R_CONST = 1.0, 0.1, 0.01

ALU = mybir.AluOpType
ACT = mybir.ActivationFunctionType
F32 = mybir.dt.float32
BF16 = mybir.dt.bfloat16
I32 = mybir.dt.int32
AX = mybir.AxisListType.X


def carry(eng, s_carry):
    eng.sem_inc(s_carry, 1)


class Chain:

    def __init__(self, eng, sem, base=0):
        self.eng, self.sem, self.base, self.n = eng, sem, base, 0

    def after(self, ins):
        self.n += 1
        ins.then_inc(self.sem, 1)
        self.eng.wait_ge(self.sem, self.base + self.n)


def build_gnn(nc, x, adj, w_gat, a_gat, w_ih_e, w_hh_e, b_ih_e, b_hh_e, w_ih_n, w_hh_n, b_ih_n, b_hh_n, out):
    N = adj.shape[0]
    GQ = N // G
    C = GQ // Q
    NB = N // P
    assert N % 2048 == 0 and x.shape[1] == D

    STRIP = 4 * BANK
    SPT = N // STRIP
    RING = 8
    TPB = RING // SPT
    LNG = min(16, C)
    BODIES = LNG // TPB
    GROUPS = C // LNG
    XG = N // BANK

    K = N // BANK
    UC = 16
    U = C // UC
    HC = UC // 2
    H = 2 * U
    RB = BANK // Q
    RAW = RB * UC * Q

    scratch = nc.dram_tensor("h_rows", (N, D), F32, kind="Internal").ap()
    stack = ExitStack()

    def sem(name):
        return stack.enter_context(nc.semaphore(name))

    def keep(name, shape, dt):
        return stack.enter_context(nc.sbuf_tensor(name, shape, dt))

    with stack:
        h = keep("h", [P, C, D], F32)
        h01 = keep("h01", [P, C, 2 * D], BF16)
        h2one = keep("h2one", [P, C, 2 * D], BF16)
        ring = keep("ring", [P, RING, STRIP], F32)
        ident = keep("ident", [P, P], F32)
        flag = keep("flag", [1, 1], I32)
        wT = keep("wT", [D, 2, D], F32)
        a12 = keep("a12", [D, 2], F32)
        wie = keep("wie", [P, 2, 3, D], F32)
        whh = keep("whh", [D, 3, 2 * D], F32)
        w2 = keep("w2", [P, 3, D], F32)
        va = keep("va", [P, 2, 2], F32)
        pick = keep("pick", [P, 1], F32)
        two = keep("two", [P, D], F32)
        dnat = keep("dnat", [P, NB], F32)
        bias = keep("bias", [P, 2, 3], F32)
        brz = keep("brz", [P, 2], F32)
        bhn = keep("bhn", [P, 1], F32)
        power = keep("power", [P, LNG], F32)

        s_carry = sem("carries_waits")

        layer0(nc, locals())
        layer1(nc, locals())


def layer0(nc, v):
    (N, GQ, C, NB, STRIP, SPT, RING, TPB, LNG, BODIES, GROUPS, XG) = (
        v[k] for k in "N GQ C NB STRIP SPT RING TPB LNG BODIES GROUPS XG".split())
    (x, adj, h, h01, h2one, ring, ident, flag, wT, a12, wie, whh, w2, va, pick, bias, brz, bhn,
     power, sem, scratch, K, U, two, dnat, s_carry) = (
        v[k] for k in ("x adj h h01 h2one ring ident flag wT a12 wie whh w2 va pick bias brz bhn "
                       "power sem scratch K U two dnat s_carry").split())

    with ExitStack() as ctx:
        def sb(name, shape, dt):
            return ctx.enter_context(nc.sbuf_tensor(name, shape, dt))

        hi2 = sb("hi2", [P, N], BF16)
        mid2 = sb("mid2", [P, N], BF16)
        low_hi = sb("low_hi", [P, N], BF16)
        hi_low = sb("hi_low", [P, N], BF16)
        xn = ring[:, 0, :].rearrange("p (b d) -> p b d", d=D)[:, 0:min(NB, STRIP // D), :]
        xn = ring[:, 0:2, :].rearrange("p r s -> p (r s)").rearrange("p (b d) -> p b d", d=D)[:, 0:NB, :]
        wstage = ring[:, 2, :].rearrange("p (a d) -> p a d", d=D)
        twice = sb("twice", [P, 2, 4, 2 * D], F32)
        rest = sb("rest", [P, 2, 2, BANK], F32)
        pair = sb("pair", [P, 2, 2, P], BF16)
        weighed = rest[:, :, :, :].rearrange("p a b n -> p (a b n)")
        below = sb("below", [P, STRIP], BF16)
        outer = sb("outer", [P, C, SPT], F32)
        neg = sb("neg", [P, C, SPT], F32)
        negmax = sb("negmax", [P, 1], F32)
        wihn = sb("wihn", [D, 3, D], F32)
        ones = sb("ones", [P, 1], F32)
        lsum = sb("lsum", [P, 4, LNG], F32)
        sq = twice[:, :, :, :].rearrange("p a b n -> p (a b n)")[:, 0:LNG * D].rearrange("p (c d) -> p c d", d=D)
        res = sb("res", [P, LNG, D], F32)
        ps = ctx.enter_context(nc.psum_tensor("ps", [P, 2, 4, BANK], F32))

        s_x = sem("x_loaded")
        s_w = sem("weights_loaded")
        s_strip = [sem(f"strip_loaded{i}") for i in range(RING)]
        s_const = sem("constants_made")
        s_id = sem("ident_made")
        s_two = sem("two_made")
        s_diag = sem("diagonal_loaded")
        s_wt = sem("weights_transposed")
        s_wk = sem("weights_kept")
        s_wp = sem("weight_products")
        s_twice_free = sem("twice_free")
        s_twice = sem("twice_ready")
        s_xt_free = sem("xt_bank_free")
        s_xt = sem("xt_transposed")
        s_hi = sem("hi_ready")
        s_rest1 = sem("rest1_ready")
        s_mid = sem("mid_ready")
        s_rest2 = sem("rest2_ready")
        s_low = sem("low_ready")
        s_hicopy = sem("hi_copied")
        s_pair_free = sem("pair_free")
        s_pair = sem("pair_ready")
        s_gram = sem("gram_ready")
        s_gram_free = sem("gram_free")
        s_relu = sem("relu_done")
        s_relu_free = sem("relu_strip_done")
        s_c = sem("vector_chain0")
        s_var = sem("variance_ready")
        s_rstd = sem("rstd_ready")
        s_ln = sem("ln_done")
        s_h0 = sem("h0_ready")
        s_r1 = sem("hrest1_ready")
        s_h1 = sem("h1_ready")
        s_r2 = sem("hrest2_ready")
        s_h2 = sem("h2_ready")
        s_neg = sem("negative_counted")
        s_ns = sem("negative_summed")
        s_flag = sem("flag_made")
        s_scr = sem("h_stored")
        gate_view = "(t n) k -> n t k"

        with nc.Block() as block:
            @block.sync
            def _(sp):
                sp.dma_start(xn, x.rearrange("(b p) d -> p b d", p=P)).then_inc(s_x, 16)
                for g in range(G):
                    sp.dma_start(h[Q * g:Q * g + Q, :, :],
                                 x[GQ * g:GQ * g + GQ, :].rearrange("(c jj) d -> jj c d", jj=Q)).then_inc(s_x, 16)

                def load(tile, strip, slot):
                    for g in range(G):
                        sp.dma_start(ring[Q * g:Q * g + Q, slot, :],
                                     adj[bass.ds(Q * tile + GQ * g, Q), STRIP * strip:STRIP * (strip + 1)]
                                     ).then_inc(s_strip[slot], 16)

                sp.wait_ge(s_twice, 2 * XG)
                sp.wait_ge(s_wt, 1)
                for slot in range(RING):
                    load(slot // SPT, slot % SPT, slot)
                with nc.allow_non_contiguous_dma(reason="the diagonal, once"):
                    sp.dma_start(dnat[:, :], adj.rearrange("i j -> (i j)")[0:N * N:N + 1].rearrange(
                        "(b p) -> p b", p=P)).then_inc(s_diag, 16)
                with sp.Fori(1, C // TPB) as body:
                    for slot in range(RING):
                        sp.wait_ge(s_gram_free, 2 + (body - 1) * RING + slot + 1)
                        carry(sp, s_carry)
                        sp.wait_ge(s_relu, (body - 1) * RING + slot + 1)
                        carry(sp, s_carry)
                        load(body * TPB + slot // SPT, slot % SPT, slot)
                with sp.Fori(0, GROUPS) as grp:
                    sp.wait_ge(s_ln, grp + 1)
                    for g in range(G):
                        sp.dma_start(scratch[bass.ds(GQ * g + grp * (Q * LNG), Q * LNG), :].rearrange(
                            "(c jj) d -> jj c d", jj=Q), h[Q * g:Q * g + Q, bass.ds(grp * LNG, LNG), :]
                        ).then_inc(s_scr, 16)
                sp.wait_ge(s_scr, 16 * G * GROUPS)
                sp.wait_ge(s_diag, 16)

            @block.gpsimd
            def _(pool):
                nc.gpsimd.memset(ident[:], 0.0).then_inc(s_id, 1)
                nc.gpsimd.memset(ones[:], 1.0).then_inc(s_const, 1)
                nc.gpsimd.memset(power[:], -0.5).then_inc(s_const, 1)
                nc.gpsimd.memset(h2one[:, :, D:2 * D], 1.0).then_inc(s_const, 1)
                nc.gpsimd.memset(pick[:], 0.0).then_inc(s_const, 1)
                pool.wait_ge(s_id, 1)
                nc.gpsimd.affine_select(out=ident[:], in_=ident[:], compare_op=ALU.not_equal, fill=1.0,
                                        base=0, pattern=[[-1, P]], channel_multiplier=1).then_inc(s_id, 1)
                pool.wait_ge(s_const, 4)
                nc.gpsimd.affine_select(out=pick[:], in_=pick[:], compare_op=ALU.not_equal, fill=1.0,
                                        base=-D, pattern=[[0, 1]], channel_multiplier=1).then_inc(s_const, 1)
                pool.wait_ge(s_const, 5)
                nc.gpsimd.memset(two[:], 0.0).then_inc(s_two, 1)
                for half in range(2):
                    pool.wait_ge(s_two, half + 1)
                    nc.gpsimd.affine_select(out=two[:], in_=two[:], compare_op=ALU.not_equal, fill=1.0,
                                            base=-D * half, pattern=[[-1, D]], channel_multiplier=1).then_inc(s_two, 1)
                pool.wait_ge(s_two, 3)
                pool.wait_ge(s_x, 16 * (1 + G))
                with pool.Fori(0, XG // 2) as pairs:
                    for s in range(2):
                        pool.wait_ge(s_twice_free, pairs * 2 + s + 1)
                        carry(pool, s_carry)
                        for dup in range(2):
                            nc.gpsimd.tensor_copy(twice[:, s, :, D * dup:D * dup + D],
                                                  xn[:, bass.ds(pairs * 8 + 4 * s, 4), :]).then_inc(s_twice, 1)
                with pool.Fori(0, GROUPS) as grp:
                    pool.wait_ge(s_var, grp + 1)
                    nc.gpsimd.tensor_tensor(out=lsum[:, 3, :], in0=lsum[:, 2, :], in1=power[:, 0:LNG],
                                            op=ALU.pow).then_inc(s_rstd, 1)

            @block.scalar
            def _(act):
                act.dma_start(wstage[0:D, 0, :], v["w_gat"]).then_inc(s_w, 16)
                for dup in range(2):
                    for m in range(2):
                        act.dma_start(wstage[0:D, 2 + 6 * m + dup:2 + 6 * m + 6:2, :],
                                      v["w_ih_e"].rearrange(gate_view, t=3)[:, :, D * m:D * m + D]).then_inc(s_w, 16)
                act.dma_start(wstage[0:D, 14:20:2, :], v["w_hh_e"].rearrange(gate_view, t=3)).then_inc(s_w, 16)
                act.dma_start(wstage[0:D, 15:20:2, :], v["w_hh_n"].rearrange(gate_view, t=3)).then_inc(s_w, 16)
                act.dma_start(wstage[0:D, 20:23, :], v["w_ih_n"].rearrange(gate_view, t=3)).then_inc(s_w, 16)
                with nc.allow_non_contiguous_dma(reason="a few hundred floats, once"):
                    act.dma_start(a12[:, :], v["a_gat"].rearrange("(m d) o -> d (m o)", m=2)).then_inc(s_w, 16)
                    for half, (ih, hh) in enumerate(((v["b_ih_e"], v["b_hh_e"]), (v["b_ih_n"], v["b_hh_n"]))):
                        for which, b in enumerate((ih, hh)):
                            act.dma_start(bias[D * half:D * half + D, which, :],
                                          b.rearrange("(t n) -> n t", t=3)).then_inc(s_w, 16)
                act.wait_ge(s_wt, 1)
                nc.scalar.copy(wT[:, 0, :], ps[0:D, 1, 0, 0:D]).then_inc(s_wk, 1)
                nc.scalar.copy(wT[:, 1, :], ps[0:D, 1, 0, 0:D]).then_inc(s_wk, 1)
                nc.scalar.copy(wie[:, :, :, :].rearrange("p m t d -> p (m t d)"),
                               ps[:, 1, 1, 0:6 * D]).then_inc(s_wk, 1)
                nc.scalar.copy(whh[:, :, :].rearrange("p t (e d) -> p (t e) d", e=2),
                               ps[0:D, 1, 2, 0:6 * D].rearrange("p (t d) -> p t d", d=D)).then_inc(s_wk, 1)
                nc.scalar.copy(wihn[:, :, :], ps[0:D, 1, 0, D:4 * D].rearrange("p (t d) -> p t d", d=D)
                               ).then_inc(s_wk, 1)
                act.wait_ge(s_wp, 1)
                nc.scalar.copy(va[:, 0, :], ps[:, 1, 3, 0:2]).then_inc(s_wk, 1)
                nc.scalar.copy(va[:, 1, 0:1], ps[:, 1, 3, 1:2]).then_inc(s_wk, 1)
                nc.scalar.copy(va[:, 1, 1:2], ps[:, 1, 3, 0:1]).then_inc(s_wk, 1)
                nc.scalar.copy(w2[D:P, :, :], ps[D:P, 1, 3, D:4 * D].rearrange("p (t d) -> p t d", d=D)
                               ).then_inc(s_wk, 1)
                with act.Fori(0, XG // 2) as pairs:
                    for s in range(2):
                        q = pairs * 2 + s
                        cols = bass.ds(pairs * (2 * BANK) + s * BANK, BANK)
                        act.wait_ge(s_xt, q + 1)
                        nc.scalar.copy(hi2[:, cols], ps[:, 0, s, :]).then_inc(s_hi, 1)
                        act.wait_ge(s_rest1, q + 1)
                        nc.scalar.copy(mid2[:, cols], rest[:, s, 0, :]).then_inc(s_mid, 1)
                        act.wait_ge(s_rest2, q + 1)
                        nc.scalar.copy(low_hi[0:D, cols], rest[0:D, s, 1, :]).then_inc(s_low, 1)
                        nc.scalar.copy(hi_low[D:P, cols], rest[D:P, s, 1, :]).then_inc(s_low, 1)

                def split_h(grp):
                    at = bass.ds(grp * LNG, LNG)
                    act.wait_ge(s_ln, grp + 1)
                    nc.scalar.copy(h01[:, at, 0:D], h[:, at, :]).then_inc(s_h0, 1)
                    act.wait_ge(s_r1, grp + 1)
                    nc.scalar.copy(h01[:, at, D:2 * D], res[:, :, :]).then_inc(s_h1, 1)
                    act.wait_ge(s_r2, grp + 1)
                    nc.scalar.copy(h2one[:, at, 0:D], res[:, :, :]).then_inc(s_h2, 1)

                def make_pair(tile, t):
                    act.wait_ge(s_pair_free, tile + 1)
                    cols = bass.ds(tile * Q, Q)
                    for part, src in ((0, hi2), (1, mid2)):
                        half = slice(D * part, D * part + D)
                        nc.scalar.copy(pair[half, t % 2, 0, :].rearrange("p (g q) -> p g q", g=G),
                                       src[half, :].rearrange("p (g m) -> p g m", g=G)[:, :, cols]).then_inc(s_pair, 1)
                    nc.scalar.copy(pair[:, t % 2, 1, :].rearrange("p (g q) -> p g q", g=G),
                                   hi_low[:, :].rearrange("p (g m) -> p g m", g=G)[:, :, cols]).then_inc(s_pair, 1)

                assert TPB % 2 == 0
                act.wait_ge(s_mid, XG)
                act.wait_ge(s_low, 2 * XG)
                act.wait_ge(s_hicopy, 2 * XG)
                with act.Fori(0, GROUPS) as grp:
                    with act.Fori(0, BODIES) as body:
                        for slot in range(RING):
                            if slot % SPT == 0:
                                make_pair(grp * LNG + body * TPB + slot // SPT, slot // SPT)
                            act.wait_ge(s_strip[slot], (grp * BODIES + body + 1) * (16 * G))
                            act.wait_ge(s_relu_free, grp * (BODIES * RING) + body * RING + slot + 1)
                            unit = grp * (LNG * SPT) + body * RING + slot
                            nc.scalar.activation(
                                below[:, :], ring[:, slot, :], ACT.Relu, scale=-1.0,
                                accum_out=neg[:, :, :].rearrange("p c s -> p (c s)")[:, bass.ds(unit, 1)]
                            ).then_inc(s_relu, 1)
                            act.wait_ge(s_relu, grp * (BODIES * RING) + body * RING + slot + 1)
                            act.sem_inc(s_relu_free, 1)
                    split_h(grp)

            @block.tensor
            def _(pe):
                pe.wait_ge(s_id, 2)
                pe.wait_ge(s_w, 16 * 13)
                id64 = ident[0:D, 0:D]
                nc.tensor.transpose(ps[0:D, 1, 0, 0:D], wstage[0:D, 0, :], id64)
                for t in range(3):
                    nc.tensor.transpose(ps[0:D, 1, 0, D * (t + 1):D * (t + 2)], wstage[0:D, 20 + t, :], id64)
                for m in range(2):
                    for t in range(3):
                        o = 3 * m + t
                        nc.tensor.transpose(ps[:, 1, 1, D * o:D * o + D],
                                            wstage[0:D, 2 + 2 * o:4 + 2 * o, :].rearrange("p a d -> p (a d)"), id64)
                for o in range(6):
                    last = nc.tensor.transpose(ps[0:D, 1, 2, D * o:D * o + D], wstage[0:D, 14 + o, :], id64)
                last.then_inc(s_wt, 1)
                pe.wait_ge(s_wk, 5)
                nc.tensor.matmul(ps[:, 1, 3, 0:2], wT[:, :, :].rearrange("p a d -> p (a d)"), a12[:, :],
                                 start=True, stop=True)
                nc.tensor.matmul(ps[D:P, 1, 3, D:4 * D], wT[:, 0, :], wihn[:, :, :].rearrange("p t d -> p (t d)"),
                                 start=True, stop=True, skip_group_check=True).then_inc(s_wp, 1)
                pe.sem_inc(s_twice_free, 2)
                pe.sem_inc(s_pair_free, 2)
                with pe.Fori(0, XG // 2) as pairs:
                    for s in range(2):
                        q = pairs * 2 + s
                        pe.wait_ge(s_twice, q * 2 + 2)
                        pe.wait_ge(s_xt_free, q + 1)
                        for b in range(4):
                            last = nc.tensor.transpose(ps[:, 0, s, P * b:P * b + P], twice[:, s, b, :], ident[:])
                        last.then_inc(s_xt, 1)
                        pe.wait_ge(s_xt, q + 1)
                        pe.sem_inc(s_twice_free, 1)
                pe.wait_ge(s_low, 2 * XG)
                pe.wait_ge(s_hicopy, 2 * XG)
                pe.wait_ge(s_wk, 9)
                with pe.Fori(0, C // TPB) as body:
                    for t in range(TPB):
                        pe.wait_ge(s_pair, (body * TPB + t) * 3 + 3)
                        for s in range(SPT):
                            strip = t * SPT + s
                            pe.wait_ge(s_gram_free, body * RING + strip + 1)
                            for b in range(4):
                                cols = slice(STRIP * s + BANK * b, STRIP * s + BANK * (b + 1))
                                o = ps[:, strip % 2, b, :]
                                nc.tensor.matmul(o, pair[:, t % 2, 0, :], hi2[:, cols], start=True, stop=False)
                                nc.tensor.matmul(o, pair[:, t % 2, 0, :], mid2[:, cols], start=False, stop=False)
                                last = nc.tensor.matmul(o, pair[:, t % 2, 1, :], low_hi[:, cols], start=False, stop=True)
                            last.then_inc(s_gram, 1)
                        pe.wait_ge(s_gram, body * RING + (t + 1) * SPT)
                        pe.sem_inc(s_pair_free, 1)
                pe.wait_ge(s_neg, 1)
                nc.tensor.matmul(ps[0:1, 0, 0, 0:1], negmax[:, :], ones[:, :], start=True, stop=True).then_inc(s_ns, 1)

            @block.vector
            def _(dve):
                dve.sem_inc(s_xt_free, 2)
                dve.sem_inc(s_gram_free, 2)
                dve.sem_inc(s_relu_free, 1)
                with dve.Fori(0, XG // 2) as pairs:
                    for s in range(2):
                        q = pairs * 2 + s
                        cols = bass.ds(pairs * (2 * BANK) + s * BANK, BANK)
                        dve.wait_ge(s_hi, q + 1)
                        nc.vector.tensor_tensor(out=rest[:, s, 0, :], in0=ps[:, 0, s, :], in1=hi2[:, cols],
                                                op=ALU.subtract).then_inc(s_rest1, 1)
                        nc.vector.tensor_copy(low_hi[D:P, cols], hi2[D:P, cols]).then_inc(s_hicopy, 1)
                        nc.vector.tensor_copy(hi_low[0:D, cols], hi2[0:D, cols]).then_inc(s_hicopy, 1)
                        dve.wait_ge(s_mid, q + 1)
                        dve.sem_inc(s_xt_free, 1)
                        nc.vector.tensor_tensor(out=rest[:, s, 1, :], in0=rest[:, s, 0, :], in1=mid2[:, cols],
                                                op=ALU.subtract).then_inc(s_rest2, 1)
                dve.wait_ge(s_w, 16 * 13)
                nc.vector.tensor_tensor(out=brz[:, :], in0=bias[:, 0, 0:2], in1=bias[:, 1, 0:2],
                                        op=ALU.add).then_inc(s_const, 1)
                nc.vector.tensor_scalar(out=bhn[:, :], in0=bias[:, 1, 2:3], scalar1=0.5, scalar2=None,
                                        op0=ALU.mult).then_inc(s_const, 1)
                dve.wait_ge(s_const, 7)
                nc.vector.tensor_scalar(out=brz[:, :], in0=brz[:, :], scalar1=0.5, scalar2=None,
                                        op0=ALU.mult).then_inc(s_const, 1)

                LN_STEPS = 7

                def norm(grp):
                    chain = Chain(dve, s_c, grp * LN_STEPS)
                    at = bass.ds(grp * LNG, LNG)
                    hg, wide = h[:, at, :], [P, LNG, D]
                    dve.wait_ge(s_gram_free, 2 + (grp + 1) * (LNG * SPT))
                    nc_sum = lsum[:, 0, :]
                    chain.after(nc.vector.tensor_reduce(nc_sum, outer[:, at, :], AX, ALU.add))
                    chain.after(nc.vector.tensor_scalar(lsum[:, 1, :], nc_sum, -R_CONST, F_CONST, ALU.mult, ALU.add))
                    chain.after(nc.vector.scalar_tensor_tensor(
                        out=sq[:, :, :], in0=hg, scalar=1.0 - B_CONST, in1=lsum[:, 1, :].unsqueeze(2).to_broadcast(wide),
                        op0=ALU.mult, op1=ALU.add))
                    chain.after(nc.vector.tensor_reduce(nc_sum, sq[:, :, :], AX, ALU.add))
                    chain.after(nc.vector.tensor_scalar(lsum[:, 1, :], nc_sum, 1.0 / D, None, ALU.mult))
                    chain.after(nc.vector.tensor_tensor(
                        out=hg, in0=sq[:, :, :], in1=lsum[:, 1, :].unsqueeze(2).to_broadcast(wide), op=ALU.subtract))
                    chain.after(nc.vector.tensor_tensor(out=sq[:, :, :], in0=hg, in1=hg, op=ALU.mult))
                    assert chain.n == LN_STEPS
                    nc.vector.tensor_reduce(nc_sum, sq[:, :, :], AX, ALU.add).then_inc(s_h1x, 1)
                    dve.wait_ge(s_h1x, grp + 1)
                    nc.vector.tensor_scalar(lsum[:, 2, :], nc_sum, 1.0 / D, EPS, ALU.mult, ALU.add).then_inc(s_var, 1)
                    dve.wait_ge(s_rstd, grp + 1)
                    nc.vector.tensor_tensor(out=hg, in0=hg, in1=lsum[:, 3, :].unsqueeze(2).to_broadcast(wide),
                                            op=ALU.mult).then_inc(s_ln, 1)
                    dve.wait_ge(s_h0, grp + 1)
                    nc.vector.tensor_tensor(out=res[:, :, :], in0=hg, in1=h01[:, at, 0:D],
                                            op=ALU.subtract).then_inc(s_r1, 1)
                    dve.wait_ge(s_h1, grp + 1)
                    nc.vector.tensor_tensor(out=res[:, :, :], in0=res[:, :, :], in1=h01[:, at, D:2 * D],
                                            op=ALU.subtract).then_inc(s_r2, 1)

                s_h1x = sem("square_sum")
                flat = outer[:, :, :].rearrange("p c s -> p (c s)")
                with dve.Fori(0, GROUPS) as grp:
                    with dve.Fori(0, BODIES) as body:
                        for slot in range(RING):
                            unit = grp * (LNG * SPT) + body * RING + slot
                            dve.wait_ge(s_strip[slot], (grp * BODIES + body + 1) * (16 * G))
                            dve.wait_ge(s_gram, unit + 1)
                            dve.wait_ge(s_gram_free, unit + 2)
                            nc.vector.scalar_tensor_tensor(
                                out=weighed[:, :], in0=ring[:, slot, :], scalar=1.0,
                                in1=ps[:, slot % 2, :, :].rearrange("p b n -> p (b n)"), op0=ALU.mult, op1=ALU.mult,
                                accum_out=flat[:, bass.ds(unit, 1)]).then_inc(s_gram_free, 1)
                    norm(grp)
                dve.wait_ge(s_relu, C * SPT)
                nc.vector.tensor_reduce(negmax[:, :], neg[:, :, :].rearrange("p c s -> p (c s)"), AX,
                                        ALU.max).then_inc(s_neg, 1)
                dve.wait_ge(s_ns, 1)
                nc.vector.tensor_scalar(flag[:, :], ps[0:1, 0, 0, 0:1], 0.0, None, ALU.is_gt).then_inc(s_flag, 1)


def layer1(nc, v):
    (N, K, adj, ident, flag, dnat) = (v[k] for k in "N K adj ident flag dnat".split())
    with ExitStack() as ctx:
        def sb(name, shape, dt):
            return ctx.enter_context(nc.sbuf_tensor(name, shape, dt))

        b = dict(v)
        b["at"] = sb("at", [P, 2, v["HC"], BANK], F32)
        b["mask"] = sb("mask", [P, 2, v["HC"], BANK], BF16)
        b["nat"] = sb("nat", [P, 4, D], F32)
        b["stage"] = sb("stage", [P, 4, 2 * D], F32)
        b["hT"] = sb("hT", [P, BANK], F32)
        b["sums"] = sb("sums", [P, 2, BANK], F32)
        b["cnt"] = sb("cnt", [P, 2, BANK], F32)
        b["wsum"] = sb("wsum", [P, 2, BANK], F32)
        b["wlow"] = sb("wlow", [P, BANK], F32)
        b["tr"] = sb("tr", [P, BANK], F32)
        b["tz"] = sb("tz", [P, BANK], F32)
        b["hn"] = sb("hn", [P, BANK], F32)
        b["nn"] = sb("nn", [P, BANK], F32)
        b["en"] = sb("en", [P, 4, 4], F32)
        b["co"] = sb("co", [P, 8, 4, 3], F32)
        b["prob"] = sb("prob", [P, 2, 4, D], F32)
        b["y"] = sb("y", [P, 4, D], F32)
        b["ysq"] = sb("ysq", [P, 4, D], F32)
        b["yo"] = sb("yo", [P, 4, D], F32)
        b["ls"] = sb("ls", [P, 4, 4], F32)
        b["not_diag"] = sb("not_diag", [P, K * v["U"], Q], F32)
        b["s_nd"] = v["sem"]("not_diag_made")
        b["ps"] = ctx.enter_context(nc.psum_tensor("ps1", [P, 8, BANK], F32))
        fast = Sweep(nc, b, "f_", 1)
        full = Sweep(nc, b, "g_", 2)
        with nc.Block() as block:
            for name in ("sync", "gpsimd", "scalar", "tensor", "vector"):
                add_engine(nc, block, name, flag, fast, full)


def add_engine(nc, block, name, flag, fast, full):
    def program(eng):
        if name == "gpsimd":
            make_not_diag(nc, eng, fast.b)
        negative = eng.value_load(flag[0:1, 0:1], min_val=0, max_val=1)
        run_fast, run_full = {
            "sync": (fast.sync, full.sync), "gpsimd": (fast.gpsimd, full.gpsimd),
            "scalar": (fast.scalar, full.scalar), "tensor": (fast.tensor, full.tensor),
            "vector": (fast.vector, full.vector)}[name]
        with eng.If(negative > 0):
            run_full(eng)
        with eng.Else():
            run_fast(eng)
    {"sync": block.sync, "gpsimd": block.gpsimd, "scalar": block.scalar, "tensor": block.tensor,
     "vector": block.vector}[name](program)


def make_not_diag(nc, pool, b):
    U = b["U"]
    nc.gpsimd.memset(b["not_diag"][:], 1.0).then_inc(b["s_nd"], 1)
    for g in range(G):
        pool.wait_ge(b["s_nd"], g + 1)
        nd = b["not_diag"][Q * g:Q * g + Q, bass.DynSlice(g * U * U, U, step=U + 1), :]
        nc.gpsimd.affine_select(out=nd, in_=nd, compare_op=ALU.not_equal, fill=0.0, base=0,
                                pattern=[[0, U], [-1, Q]], channel_multiplier=1).then_inc(b["s_nd"], 1)
    pool.wait_ge(b["s_nd"], G + 1)


ACC_T, ACC_S, ACC_C = 0, 1, 2
R, Z, IN, HN, MISC = 3, 4, 5, 6, 7


class Sweep:

    SEMS = ("raw0 raw1 diag turned split mask_ready t_done s_done sums_copied cnt_copied "
            "s_evac t_evac small ekb expd expa kbb scaled stage_ready ht_ps ht_ready gates tr tz hn g2 nn u "
            "back y_read var rstd yout stored nat_in nat_free stage_free chain")

    def __init__(self, nc, b, prefix, signs):
        self.nc, self.b, self.signs = nc, b, signs
        self.s = {n: b["sem"](prefix + n) for n in self.SEMS.split()}
        self.N, self.K, self.U, self.H = b["N"], b["K"], b["U"], b["H"]
        self.GQ = b["GQ"]

    def where(self, position):
        return min(position, self.H)

    def products_done(self, k):
        return (k + 1) * (self.H * self.signs) + (self.signs - 1)

    def sync(self, sp):
        nc, b, s = self.nc, self.b, self.s
        ring = b["ring"][:, :, :].rearrange("p (n r) m -> p n (r m)", n=2)
        U, GQ, RB, UC = self.U, self.GQ, b["RB"], b["UC"]

        def unit(k, u):
            n = k * U + u
            raw = ring[:, (u if U > 1 else 0) % 2, :].rearrange("p (f m) -> p f m", f=RB)
            for g in range(G):
                sp.dma_start(
                    raw[Q * g:Q * g + Q, :, :],
                    b["adj"][bass.ds(k * BANK, BANK), GQ * g + UC * Q * u:GQ * g + UC * Q * (u + 1)].rearrange(
                        "(f ii) m -> ii f m", ii=Q)).then_inc(s[f"raw{u % 2}"], 16)

        slots = min(2, U)
        for u in range(U):
            if u >= slots:
                sp.wait_ge(s["turned"], 2 * (u + 1 - slots))
            unit(0, u)
        with sp.Fori(1, self.K) as k:
            for u in range(U):
                sp.wait_ge(s["turned"], k * (2 * U) + 2 * (u + 1 - slots))
                unit(k, u)

    def gpsimd(self, pool):
        nc, b, s = self.nc, self.b, self.s
        U, RB, UC, K = self.U, b["RB"], b["UC"], self.K
        ring = b["ring"][:, :, :].rearrange("p (n r) m -> p n (r m)", n=2)
        slots = min(2, U)

        def no_diagonal(k):
            for u in range(U):
                raw = ring[:, u % 2, :].rearrange("p (f m) -> p f m", f=RB)
                diag = bass.AP(tensor=raw.tensor, offset=raw.offset,
                               ap=[list(raw.ap[0]), [UC * Q + Q, RB], [1, Q]])
                pool.wait_ge(s[f"raw{u % 2}"], (k * ((U + 1 - u % 2) // 2) + u // 2 + 1) * (16 * G))
                nc.gpsimd.tensor_tensor(
                    out=diag, in0=diag,
                    in1=b["not_diag"][:, bass.ds(k * U + u, 1), :].to_broadcast([P, RB, Q]),
                    op=ALU.mult).then_inc(s["diag"], 1)

        def rows(k):
            pool.wait_ge(s["nat_in"], k * 16 + 16)
            pool.wait_ge(s["stage_free"], k + 1)
            carry(pool, b["s_carry"])
            for dup in range(2):
                nc.gpsimd.tensor_copy(b["stage"][:, :, D * dup:D * dup + D],
                                      b["nat"][:, :, :]).then_inc(s["stage_ready"], 1)

        def end(k):
            pool.wait_ge(s["var"], k + 1)
            nc.gpsimd.tensor_tensor(out=b["ls"][:, 3, :], in0=b["ls"][:, 2, :], in1=b["power"][:, 0:4],
                                    op=ALU.pow).then_inc(s["rstd"], 1)

        if self.signs == 2:
            with pool.Fori(0, K) as k:
                no_diagonal(k)
                rows(k)
                end(k)
        else:
            no_diagonal(0)
            with pool.Fori(1, K) as k:
                rows(k - 1)
                no_diagonal(k)
                end(k - 1)
            rows(K - 1)
            end(K - 1)

    def vector(self, dve):
        nc, b, s, ps = self.nc, self.b, self.s, self.b["ps"]
        H, HC, RB, UC, K, N, signs = self.H, b["HC"], b["RB"], b["UC"], self.K, self.N, self.signs
        ring = b["ring"][:, :, :].rearrange("p (n r) m -> p n (r m)", n=2)
        hi = slice(D, P)

        def turn(k, half, first):
            n = k * H + half
            u, part = half // 2, half % 2
            if part == 0:
                dve.wait_ge(s["diag"], k * self.U + u + 1)
            slot = part if signs == 1 else 0
            if signs == 1:
                if not (first and half < 2):
                    dve.wait_ge(s["t_done"], n - 1)
                    dve.wait_ge(s["mask_ready"], n - 1)
            raw = ring[:, u % 2, 0:RB * UC * Q].rearrange("p (f c q) -> p f c q", f=RB, q=Q)
            nc.vector.transpose(
                b["at"][:, slot, :, :].rearrange("p c (f q) -> p f c q", q=Q),
                raw[:, :, HC * part:HC * part + HC, :]).then_inc(s["turned"], 1)
            if signs == 2:
                dve.wait_ge(s["turned"], n + 1)
                for i, sign in enumerate((1.0, -1.0)):
                    m = n * 2 + i
                    dve.wait_ge(s["s_done"], m + 1)
                    dve.wait_ge(s["t_done"], m + 1)
                    nc.vector.tensor_scalar(b["at"][:, 1, :, :], b["at"][:, 0, :, :], sign, 0.0,
                                            ALU.mult, ALU.max).then_inc(s["split"], 1)
                    nc.vector.tensor_scalar(b["mask"][:, 0, :, :], b["at"][:, 0, :, :], sign, 0.0,
                                            ALU.mult, ALU.is_gt).then_inc(s["mask_ready"], 1)
                    dve.wait_ge(s["split"], m + 1)
                    dve.wait_ge(s["mask_ready"], m + 1)

        CHAIN = {1: 25, 2: 34}[signs]

        def evac(k, c):
            dve.wait_ge(s["s_done"], self.products_done(k))
            for i in range(signs):
                c.after(nc.vector.tensor_copy(b["wlow"][hi, :], ps[0:D, 3 * i + ACC_T, :]))
                c.after(nc.vector.tensor_tensor(out=b["wsum"][hi, i, :], in0=ps[hi, 3 * i + ACC_T, :],
                                                in1=b["wlow"][hi, :], op=ALU.add))
            dve.wait_ge(s["sums_copied"], (k + 1) * signs)
            for i in range(signs):
                nc.vector.tensor_tensor(out=b["sums"][0:D, i, :], in0=ps[0:D, 3 * i + ACC_C, :],
                                        in1=b["sums"][0:D, i, :], op=ALU.add).then_inc(s["s_evac"], 1)

        def softmax(k, c):
            en, co = b["en"], b["co"]
            logit, count = en[:, :, 0:signs], en[:, :, 2:2 + signs]
            col = lambda j, w=signs: co[:, j, :, 0:w]
            dve.wait_ge(s["small"], k + 1)
            for part in (0, 2):
                c.after(nc.vector.tensor_copy(
                    en[:, :, part:part + signs],
                    ps[:, HN, 0:16].rearrange("p (b e) -> p b e", b=4)[:, :, part:part + signs]))
            c.after(nc.vector.scalar_tensor_tensor(out=col(0), in0=logit, scalar=ALPHA, in1=logit,
                                                   op0=ALU.mult, op1=ALU.max))
            c.after(nc.vector.tensor_scalar(col(1), count, 0.0, None, ALU.is_gt))
            c.after(nc.vector.tensor_tensor(out=col(0), in0=col(0), in1=col(1), op=ALU.mult))
            c.after(nc.vector.tensor_scalar(col(1), col(1), -1.0, -NEG_INF, ALU.add, ALU.mult))
            c.after(nc.vector.tensor_tensor(out=col(0), in0=col(0), in1=col(1), op=ALU.add))
            if signs == 2:
                c.after(nc.vector.tensor_tensor(out=co[:, 2, :, 0], in0=co[:, 0, :, 0], in1=co[:, 0, :, 1],
                                                op=ALU.max))
                c.after(nc.vector.tensor_scalar(co[:, 2, :, 0], co[:, 2, :, 0], NEG_INF, None, ALU.max))
            else:
                c.after(nc.vector.tensor_scalar(co[:, 2, :, 0], co[:, 0, :, 0], NEG_INF, None, ALU.max))
            for i in range(signs):
                c.after(nc.vector.tensor_tensor(out=co[:, 3, :, i], in0=co[:, 0, :, i], in1=co[:, 2, :, 0],
                                                op=ALU.subtract))
            nc.vector.tensor_scalar(co[:, 3, :, signs], co[:, 2, :, 0], -1.0, NEG_INF, ALU.mult,
                                    ALU.add).then_inc(s["expa"], 1)
            if signs == 2:
                c.after(nc.vector.tensor_tensor(out=co[:, 5, :, 0], in0=en[:, :, 2], in1=en[:, :, 3], op=ALU.add))
                c.after(nc.vector.tensor_scalar(en[:, :, 2 + signs] if signs == 1 else co[:, 5, :, 2],
                                                co[:, 5, :, 0], -1.0, float(N), ALU.mult, ALU.add))
                zeros = co[:, 5, :, 2]
            else:
                c.after(nc.vector.tensor_scalar(co[:, 5, :, 2], en[:, :, 2], -1.0, float(N), ALU.mult, ALU.add))
                zeros = co[:, 5, :, 2]
            dve.wait_ge(s["expd"], k + 1)
            c.after(nc.vector.tensor_tensor(out=co[:, 6, :, 0:signs], in0=co[:, 4, :, 0:signs], in1=count,
                                            op=ALU.mult))
            c.after(nc.vector.tensor_tensor(out=co[:, 6, :, 2], in0=co[:, 4, :, signs], in1=zeros, op=ALU.mult))
            for i in range(signs):
                c.after(nc.vector.tensor_tensor(out=co[:, 6, :, 2], in0=co[:, 6, :, 2], in1=co[:, 6, :, i],
                                                op=ALU.add))
            c.after(nc.vector.reciprocal(co[:, 7, :, 0], co[:, 6, :, 2]))
            for i in range(signs):
                c.after(nc.vector.tensor_tensor(out=co[:, 7, :, 1 + i], in0=co[:, 4, :, i], in1=co[:, 7, :, 0],
                                                op=ALU.mult))
                nc.vector.tensor_copy(b["prob"][:, i, :, :],
                                      co[:, 7, :, 1 + i:2 + i].to_broadcast([P, 4, D])).then_inc(s["ekb"], 1)

        def scale(k, c):
            dve.wait_ge(s["kbb"], k + 1)
            if signs == 2:
                c.after(nc.vector.tensor_tensor(out=b["wsum"][hi, 1, :], in0=ps[hi, R, :], in1=b["wsum"][hi, 1, :],
                                                op=ALU.mult))
                c.after(nc.vector.tensor_tensor(out=b["wsum"][hi, 0, :], in0=ps[hi, IN, :], in1=b["wsum"][hi, 0, :],
                                                op=ALU.mult))
                nc.vector.tensor_tensor(out=b["wsum"][hi, 0, :], in0=b["wsum"][hi, 0, :], in1=b["wsum"][hi, 1, :],
                                        op=ALU.subtract).then_inc(s["scaled"], 1)
            else:
                nc.vector.tensor_tensor(out=b["wsum"][hi, 0, :], in0=ps[hi, IN, :], in1=b["wsum"][hi, 0, :],
                                        op=ALU.mult).then_inc(s["scaled"], 1)

        def reset(k, c):
            dve.wait_ge(s["tr"], k + 1)
            dve.wait_ge(s["hn"], k + 1)
            c.after(nc.vector.scalar_tensor_tensor(out=b["hn"][:, :], in0=b["tr"][:, :], scalar=1.0,
                                                   in1=b["hn"][:, :], op0=ALU.add, op1=ALU.mult))
            nc.vector.tensor_tensor(out=b["hn"][:, :], in0=ps[:, IN, :], in1=b["hn"][:, :],
                                    op=ALU.add).then_inc(s["g2"], 1)

        def update(k, c):
            dve.wait_ge(s["nn"], k + 1)
            dve.wait_ge(s["ht_ready"], k + 1)
            dve.wait_ge(s["tz"], k + 1)
            c.after(nc.vector.tensor_tensor(out=b["hT"][:, :], in0=b["hT"][:, :], in1=b["nn"][:, :],
                                            op=ALU.subtract))
            c.after(nc.vector.scalar_tensor_tensor(out=b["tz"][:, :], in0=b["tz"][:, :], scalar=1.0,
                                                   in1=b["hT"][:, :], op0=ALU.add, op1=ALU.mult))
            nc.vector.scalar_tensor_tensor(out=b["hT"][:, :], in0=b["tz"][:, :], scalar=0.5, in1=b["nn"][:, :],
                                           op0=ALU.mult, op1=ALU.add).then_inc(s["u"], 1)

        def norm(k, c):
            y, ls, wide = b["y"], b["ls"], [P, 4, D]
            dve.wait_ge(s["back"], k + 1)
            nc.vector.tensor_tensor(
                out=y[:, :, :], in0=ps[:, MISC, 0:4 * D].rearrange("p (b d) -> p b d", d=D),
                in1=b["dnat"][:, bass.ds(k * 4, 4)].unsqueeze(2).to_broadcast(wide), op=ALU.mult).then_inc(s["y_read"], 1)
            dve.wait_ge(s["y_read"], k + 2)
            nc.vector.tensor_tensor(out=y[:, :, :], in0=y[:, :, :], in1=b["nat"][:, :, :],
                                    op=ALU.add).then_inc(s["nat_free"], 1)
            dve.wait_ge(s["nat_free"], k + 2)
            c.after(nc.vector.tensor_reduce(ls[:, 0, :], y[:, :, :], AX, ALU.add))
            c.after(nc.vector.tensor_scalar(ls[:, 1, :], ls[:, 0, :], 1.0 / D, None, ALU.mult))
            c.after(nc.vector.tensor_tensor(out=y[:, :, :], in0=y[:, :, :],
                                            in1=ls[:, 1, :].unsqueeze(2).to_broadcast(wide), op=ALU.subtract))
            c.after(nc.vector.tensor_tensor(out=b["ysq"][:, :, :], in0=y[:, :, :], in1=y[:, :, :], op=ALU.mult))
            c.after(nc.vector.tensor_reduce(ls[:, 0, :], b["ysq"][:, :, :], AX, ALU.add))
            nc.vector.tensor_scalar(ls[:, 2, :], ls[:, 0, :], 1.0 / D, EPS, ALU.mult, ALU.add).then_inc(s["var"], 1)

        def result(k, c):
            dve.wait_ge(s["rstd"], k + 1)
            dve.wait_ge(s["stored"], k * 16 + 16)
            nc.vector.tensor_tensor(out=b["yo"][:, :, :], in0=b["y"][:, :, :],
                                    in1=b["ls"][:, 3, :].unsqueeze(2).to_broadcast([P, 4, D]),
                                    op=ALU.mult).then_inc(s["yout"], 1)

        dve.sem_inc(s["y_read"], 1)
        dve.sem_inc(s["nat_free"], 1)
        dve.sem_inc(s["stored"], 16)
        steps = ((evac, 1), (softmax, 2), (scale, 3), (reset, 5), (update, 6), (norm, 7), (result, 8))
        self.weave(dve, turn, steps, CHAIN)

    def weave(self, eng, half_step, steps, chain_length=None):
        def run(k, first, prev):
            chain = None if prev is None or chain_length is None else Chain(eng, self.s["chain"], prev * chain_length)

            def at(position):
                for step, where in steps:
                    if prev is not None and self.where(where) == position:
                        step(prev, chain)

            for half in range(self.H):
                at(half)
                if k is not None:
                    half_step(k, half, first)
            at(self.H)
            if chain is not None and chain.n != chain_length:
                raise AssertionError(chain.n)

        if self.signs == 2:
            for k, first in ((0, True), (None, False)):
                if first:
                    run(0, True, None)
                    run(None, False, 0)
                else:
                    with eng.Fori(1, self.K) as i:
                        run(i, False, None)
                        run(None, False, i)
        else:
            run(0, True, None)
            with eng.Fori(1, self.K) as i:
                run(i, False, i - 1)
            run(None, False, self.K - 1)

    def scalar(self, act):
        nc, b, s, ps = self.nc, self.b, self.s, self.b["ps"]
        H, signs = self.H, self.signs
        hi = slice(D, P)

        def sign(k, half, first):
            if signs == 2:
                return
            n = k * H + half
            act.wait_ge(s["turned"], n + 1)
            if not (first and half < 2):
                act.wait_ge(s["s_done"], n - 1)
            nc.scalar.activation(b["mask"][:, half % 2, :, :], b["at"][:, half % 2, :, :],
                                 ACT.Sign).then_inc(s["mask_ready"], 1)

        def evac(k, c):
            act.wait_ge(s["s_done"], self.products_done(k))
            for i in range(signs):
                nc.scalar.copy(b["sums"][:, i, :], ps[:, 3 * i + ACC_S, :]).then_inc(s["sums_copied"], 1)
                nc.scalar.copy(b["cnt"][hi, i, :], ps[hi, 3 * i + ACC_C, :]).then_inc(s["cnt_copied"], 1)
            act.wait_ge(s["ht_ps"], k + 1)
            nc.scalar.copy(b["hT"][:, :], ps[:, MISC, :]).then_inc(s["ht_ready"], 1)

        def exps(k, c):
            act.wait_ge(s["expa"], k + 1)
            nc.scalar.activation(b["co"][:, 4, :, 0:signs + 1], b["co"][:, 3, :, 0:signs + 1],
                                 ACT.Exp).then_inc(s["expd"], 1)

        def gates(k, c):
            act.wait_ge(s["gates"], k + 1)
            nc.scalar.activation(b["tr"][:, :], ps[:, R, :], ACT.Tanh, bias=b["brz"][:, 0:1],
                                 scale=0.5).then_inc(s["tr"], 1)
            nc.scalar.activation(b["hn"][:, :], ps[:, HN, :], ACT.Identity, bias=b["bhn"][:, 0:1],
                                 scale=0.5).then_inc(s["hn"], 1)
            nc.scalar.activation(b["tz"][:, :], ps[:, Z, :], ACT.Tanh, bias=b["brz"][:, 1:2],
                                 scale=0.5).then_inc(s["tz"], 1)

        def new(k, c):
            act.wait_ge(s["g2"], k + 1)
            nc.scalar.activation(b["nn"][:, :], b["hn"][:, :], ACT.Tanh,
                                 bias=b["bias"][:, 0, 2:3]).then_inc(s["nn"], 1)

        def rows(k, c):
            act.wait_ge(s["nat_free"], k + 1)
            act.dma_start(b["nat"][:, :, :], b["scratch"][bass.ds(k * BANK, BANK), :].rearrange(
                "(b p) d -> p b d", p=P)).then_inc(s["nat_in"], 16)

        def store(k, c):
            act.wait_ge(s["yout"], k + 1)
            act.dma_start(b["out"][bass.ds(k * BANK, BANK), :].rearrange("(b p) d -> p b d", p=P),
                          b["yo"][:, :, :]).then_inc(s["stored"], 16)

        self.weave(act, sign, ((rows, 0), (evac, 1), (exps, 2), (gates, 4), (new, 5), (store, 8)))
        act.wait_ge(s["stored"], 16 * (self.K + 1))

    def tensor(self, pe):
        nc, b, s, ps = self.nc, self.b, self.s, self.b["ps"]
        H, HC, signs = self.H, b["HC"], self.signs
        hi = slice(D, P)
        h, h01, h2one = b["h"], b["h01"], b["h2one"]
        mm = nc.tensor.matmul

        def products(k, half, first):
            for i in range(signs):
                n = (k * H + half) * signs + i
                slot = half % 2 if signs == 1 else 1
                mslot = half % 2 if signs == 1 else 0
                if half == 0 and i == 0 and not first:
                    pe.wait_ge(s["s_evac"], k * signs)
                    pe.wait_ge(s["cnt_copied"], k * signs)
                pe.wait_ge(s["turned" if signs == 1 else "split"], n + 1)
                for cl in range(HC):
                    c = half * HC + cl
                    o = ps[D * (cl % 2):D * (cl % 2) + D, 3 * i + ACC_T, :]
                    last = mm(o, h[:, c, :], b["at"][:, slot, cl, :], start=c < 2, stop=c >= H * HC - 2)
                last.then_inc(s["t_done"], 1)
                pe.wait_ge(s["mask_ready"], n + 1)
                for cl in range(HC):
                    c = half * HC + cl
                    ends = dict(start=c == 0, stop=c == H * HC - 1)
                    mm(ps[:, 3 * i + ACC_S, :], h01[:, c, :], b["mask"][:, mslot, cl, :], **ends)
                    last = mm(ps[:, 3 * i + ACC_C, :], h2one[:, c, :], b["mask"][:, mslot, cl, :], **ends)
                last.then_inc(s["s_done"], 1)

        def turn_h(k, c):
            pe.wait_ge(s["stage_ready"], k * 2 + 2)
            pe.wait_ge(s["y_read"], k + 1)
            for i in range(4):
                last = nc.tensor.transpose(ps[:, MISC, P * i:P * i + P], b["stage"][:, i, :], b["ident"][:])
            last.then_inc(s["ht_ps"], 1)
            pe.wait_ge(s["ht_ps"], k + 1)
            pe.sem_inc(s["stage_free"], 1)

        def small(k, c):
            pe.wait_ge(s["s_evac"], (k + 1) * signs)
            pe.wait_ge(s["cnt_copied"], (k + 1) * signs)
            en = ps[:, HN, 0:16].rearrange("p (b e) -> p b e", b=4)
            for q in range(4):
                cols = slice(P * q, P * q + P)
                for i in range(signs):
                    mm(en[:, q, 0:signs], b["sums"][:, i, cols], b["va"][:, i, 0:signs],
                       start=i == 0, stop=i == signs - 1)
                for i in range(signs):
                    last = mm(en[:, q, 2 + i:3 + i], b["cnt"][hi, i, cols], b["pick"][hi, :], start=True, stop=True)
            last.then_inc(s["small"], 1)

        def spread(k, c):
            pe.wait_ge(s["ekb"], (k + 1) * signs)
            for i in range(signs):
                for q in range(4):
                    last = mm(ps[hi, (IN, R)[i], P * q:P * q + P], b["prob"][:, i, q, :], b["ident"][:, :],
                              start=True, stop=True)
            last.then_inc(s["kbb"], 1)

        def gates(k, c):
            pe.wait_ge(s["ht_ready"], k + 1)
            pe.wait_ge(s["scaled"], k + 1)
            for t, bank in ((0, R), (2, HN), (1, Z)):
                mm(ps[:, bank, :], b["whh"][:, t, :], b["hT"][0:D, :], start=True, stop=t == 2, skip_group_check=True)
            for t, bank in ((0, R), (2, IN), (1, Z)):
                for i in range(signs):
                    mm(ps[0:D, bank, :], b["wie"][:, i, t, :], b["sums"][:, i, :], start=t == 2 and i == 0,
                       stop=i == signs - 1, skip_group_check=True)
                last = mm(ps[hi, bank, :], b["w2"][hi, t, :], b["wsum"][hi, 0, :], start=t == 2, stop=True,
                          skip_group_check=True)
            last.then_inc(s["gates"], 1)

        def back(k, c):
            pe.wait_ge(s["u"], k + 1)
            for q in range(4):
                last = mm(ps[:, MISC, D * q:D * q + D], b["hT"][:, P * q:P * q + P], b["two"][:, :],
                          start=True, stop=True)
            last.then_inc(s["back"], 1)

        pe.sem_inc(s["stage_free"], 1)
        if signs == 2:
            pe.sem_inc(s["t_done"], 1)
            pe.sem_inc(s["s_done"], 1)
        self.weave(pe, products, ((turn_h, 0), (small, 1), (spread, 2), (gates, 3), (back, 6)))


_INS = ["x", "adj", "L1_gnn_W_gat", "L1_gnn_a_gat", "L1_gnn_w_ih_e", "L1_gnn_w_hh_e", "L1_gnn_b_ih_e",
        "L1_gnn_b_hh_e", "L1_gnn_w_ih_n", "L1_gnn_w_hh_n", "L1_gnn_b_ih_n", "L1_gnn_b_hh_n"]


def kernel(**inputs):
    import numpy as _np
    import concourse.bacc as _bacc
    from concourse import mybir as _mybir
    from concourse.bass_utils import run_bass_kernel_spmd as _run

    nc = _bacc.Bacc("TRN2", target_bir_lowering=False, num_devices=1)
    arrays, args = {}, []
    for name in _INS:
        a = _np.ascontiguousarray(inputs[name])
        arrays[f"in_{name}"] = a
        args.append(nc.dram_tensor(f"in_{name}", a.shape, _mybir.dt.from_np(a.dtype), kind="ExternalInput").ap())
    shape = inputs["x"].shape
    out = nc.dram_tensor("out_0", shape, _mybir.dt.float32, kind="ExternalOutput").ap()
    build_gnn(nc, *args, out)
    return _run(nc, [arrays], core_ids=[0]).results[0]["out_0"]
```

```python
from contextlib import ExitStack

import concourse.bass as bass
from concourse import mybir

P = 128
Q = 32
G = P // Q
BANK = 512
D = 64
EPS = 1e-5
ALPHA = 0.2
NEG_INF = -9000000000000000.0
F_CONST, B_CONST, R_CONST = 1.0, 0.1, 0.01

ALU = mybir.AluOpType
ACT = mybir.ActivationFunctionType
F32 = mybir.dt.float32
BF16 = mybir.dt.bfloat16
F32R = mybir.dt.float32r
U32 = mybir.dt.uint32
I32 = mybir.dt.int32
AX = mybir.AxisListType.X


def carry(eng, s_carry):
    eng.sem_inc(s_carry, 1)


class Chain:

    def __init__(self, eng, sem, base=0):
        self.eng, self.sem, self.base, self.n = eng, sem, base, 0

    def after(self, ins):
        self.n += 1
        ins.then_inc(self.sem, 1)
        self.eng.wait_ge(self.sem, self.base + self.n)


def build_gnn(nc, x, adj, w_gat, a_gat, w_ih_e, w_hh_e, b_ih_e, b_hh_e, w_ih_n, w_hh_n, b_ih_n, b_hh_n, out):
    N = adj.shape[0]
    GQ = N // G
    C = GQ // Q
    NB = N // P
    assert N % 2048 == 0 and x.shape[1] == D

    STRIP = 4 * BANK
    SPT = N // STRIP
    RING = 8
    TPB = RING // SPT
    LNG = min(8, C)
    BODIES = LNG // TPB
    GROUPS = C // LNG
    XG = C // 4

    K = N // BANK
    UC = 8
    U = C // UC
    SLOTS = min(4, U)
    HC = UC // 2
    H = 2 * U
    RB = BANK // Q
    RAW = RB * UC * Q

    scratch = nc.dram_tensor("h_rows", (N, D + 1), F32, kind="Internal").ap()
    stack = ExitStack()

    def sem(name):
        return stack.enter_context(nc.semaphore(name))

    def keep(name, shape, dt):
        return stack.enter_context(nc.sbuf_tensor(name, shape, dt))

    with stack:
        h = keep("h", [P, C, D + 1], F32)
        parts = keep("parts", [P, C, 2, D], F32R)
        ones = keep("ones", [P, P], F32R)
        one = keep("one", [P, 1], F32)
        ring = keep("ring", [P, RING, STRIP], F32)
        ident = keep("ident", [P, P], F32)
        flag = keep("flag", [1, 1], I32)
        wT = keep("wT", [D, 2, D], F32)
        a12 = keep("a12", [D, 2], F32)
        wie = keep("wie", [P, 2, 3, D], F32)
        whh = keep("whh", [D, 3, 2 * D], F32)
        w2 = keep("w2", [P, 3, D], F32)
        w_edge = keep("w_edge", [P, 2, D], F32)
        w_node = keep("w_node", [P, 2, D], F32)
        va = keep("va", [P, 2, 2], F32)
        pick = keep("pick", [P, 1], F32)
        two = keep("two", [P, D], F32)
        dnat = keep("dnat", [P, NB], F32)
        bias = keep("bias", [P, 2, 3], F32)
        brz = keep("brz", [P, 2], F32)
        bhn = keep("bhn", [P, 1], F32)
        not_diag = keep("not_diag", [P, K * U // 2, Q], F32)
        power = keep("power", [P, LNG], F32)

        s_carry = sem("carries_waits")
        s_nd = sem("not_diag_made")
        s_scr = sem("h_stored")
        s_raw = {prefix: [sem(f"{prefix}unit_loaded{i}") for i in range(SLOTS)] for prefix in ("f_", "g_")}

        v = dict(locals())
        layer0(nc, v)
        layer1(nc, v)


def load_unit(sp, v, prefix, k, u):
    RB, UC, GQ, slot = v["RB"], v["UC"], v["GQ"], u % v["SLOTS"]
    raw = unit_view(v, slot).rearrange("p (f m) -> p f m", f=RB)
    for g in range(G):
        sp.dma_start(
            raw[Q * g:Q * g + Q, :, :],
            v["adj"][bass.ds(k * BANK, BANK), GQ * g + UC * Q * u:GQ * g + UC * Q * (u + 1)].rearrange(
                "(f ii) m -> ii f m", ii=Q)).then_inc(v["s_raw"][prefix][slot], 16)


def unit_view(v, slot):
    return v["ring"][:, 2 * slot:2 * slot + 2, :].rearrange("p r m -> p (r m)")


def layer0(nc, v):
    (N, GQ, C, NB, STRIP, SPT, RING, TPB, LNG, BODIES, GROUPS, XG) = (
        v[k] for k in "N GQ C NB STRIP SPT RING TPB LNG BODIES GROUPS XG".split())
    (x, adj, h, parts, ones, one, ring, ident, flag, wT, a12, wie, whh, w2, va, pick, bias, brz, bhn,
     power, sem, scratch, K, U, two, dnat, s_carry) = (
        v[k] for k in ("x adj h parts ones one ring ident flag wT a12 wie whh w2 va pick bias brz bhn "
                       "power sem scratch K U two dnat s_carry").split())

    with ExitStack() as ctx:
        def sb(name, shape, dt):
            return ctx.enter_context(nc.sbuf_tensor(name, shape, dt))

        high2 = sb("high2", [P, N], F32R)
        low2 = sb("low2", [P, N], F32R)
        pair = sb("pair", [P, 2, P], F32R)
        weighed = sb("weighed", [P, STRIP], F32)
        wstage = weighed[:, :].rearrange("p (a d) -> p a d", d=D)
        signs = sb("signs", [P, STRIP], BF16)
        outer = sb("outer", [P, C, SPT], F32)
        rowsign = sb("rowsign", [P, C, SPT], F32)
        wihn = sb("wihn", [D, 3, D], F32)
        lsum = sb("lsum", [P, 4, LNG], F32)
        sq = weighed[:, 0:LNG * D].rearrange("p (c d) -> p c d", d=D)
        ps = ctx.enter_context(nc.psum_tensor("ps", [P, 2, 4, BANK], F32))

        s_x = sem("x_loaded")
        s_w = sem("weights_loaded")
        s_strip = [sem(f"strip_loaded{i}") for i in range(RING)]
        s_const = sem("constants_made")
        s_bias = sem("biases_made")
        s_id = sem("ident_made")
        s_two = sem("two_made")
        s_diag = sem("diagonal_loaded")
        s_wt = sem("weights_transposed")
        s_wk = sem("weights_kept")
        s_wp = sem("weight_products")
        s_xt = sem("xt_transposed")
        s_hi = sem("hi_ready")
        s_low = sem("low_ready")
        s_pair_free = sem("pair_free")
        s_pair = sem("pair_ready")
        s_gram = sem("gram_ready")
        s_gram_free = sem("gram_free")
        s_sign = sem("signs_summed")
        s_sign_free = sem("sign_strip_done")
        s_c = sem("vector_chain0")
        s_var = sem("variance_ready")
        s_rstd = sem("rstd_ready")
        s_ln = sem("ln_done")
        s_h0 = sem("h_high_ready")
        s_h1 = sem("h_low_ready")
        s_scr = v["s_scr"]
        gate_view = "(t n) k -> n t k"

        def blocks(part, c):
            return part[:, :].rearrange("p (g c q) -> p c g q", g=G, q=Q)[:, bass.ds(c, 4), :, :]

        def banked(i):
            return ps[:, 0, i, :].rearrange("p (c g q) -> p c g q", c=4, g=G)

        with nc.Block() as block:
            @block.sync
            def _(sp):
                for g in range(G):
                    sp.dma_start(h[Q * g:Q * g + Q, :, 1:],
                                 x[GQ * g:GQ * g + GQ, :].rearrange("(c jj) d -> jj c d", jj=Q)).then_inc(s_x, 16)

                def load(tile, strip, slot):
                    for g in range(G):
                        sp.dma_start(ring[Q * g:Q * g + Q, slot, :],
                                     adj[bass.ds(Q * tile + GQ * g, Q), STRIP * strip:STRIP * (strip + 1)]
                                     ).then_inc(s_strip[slot], 16)

                for slot in range(RING):
                    load(slot // SPT, slot % SPT, slot)
                with nc.allow_non_contiguous_dma(reason="the diagonal, once"):
                    sp.dma_start(dnat[:, :], adj.rearrange("i j -> (i j)")[0:N * N:N + 1].rearrange(
                        "(b p) -> p b", p=P)).then_inc(s_diag, 16)
                with sp.Fori(1, C // TPB) as body:
                    for slot in range(RING):
                        sp.wait_ge(s_gram_free, 2 + (body - 1) * RING + slot + 1)
                        carry(sp, s_carry)
                        sp.wait_ge(s_sign, (body - 1) * RING + slot + 1)
                        carry(sp, s_carry)
                        load(body * TPB + slot // SPT, slot % SPT, slot)
                for u in range(v["SLOTS"]):
                    sp.wait_ge(s_gram_free, 2 + C * SPT - RING + 2 * (u + 1))
                    sp.wait_ge(s_sign, C * SPT - RING + 2 * (u + 1))
                    load_unit(sp, v, "f_", 0, u)
                sp.wait_ge(s_diag, 16)

            @block.gpsimd
            def _(pool):
                nc.gpsimd.memset(ident[:], 0.0).then_inc(s_id, 1)
                nc.gpsimd.memset(one[:], 1.0).then_inc(s_const, 1)
                nc.gpsimd.memset(power[:], -0.5).then_inc(s_const, 1)
                nc.gpsimd.memset(pick[:], 0.0).then_inc(s_const, 1)
                pool.wait_ge(s_id, 1)
                nc.gpsimd.affine_select(out=ident[:], in_=ident[:], compare_op=ALU.not_equal, fill=1.0,
                                        base=0, pattern=[[-1, P]], channel_multiplier=1).then_inc(s_id, 1)
                pool.wait_ge(s_id, 2)
                nc.gpsimd.tensor_scalar(ones[:, :], ident[:, :], 0.0, 1.0, ALU.mult, ALU.add).then_inc(s_const, 1)
                pool.wait_ge(s_const, 4)
                nc.gpsimd.affine_select(out=pick[:], in_=pick[:], compare_op=ALU.not_equal, fill=1.0,
                                        base=0, pattern=[[0, 1]], channel_multiplier=1).then_inc(s_const, 1)
                pool.wait_ge(s_const, 5)
                nc.gpsimd.memset(two[:], 0.0).then_inc(s_two, 1)
                for half in range(2):
                    pool.wait_ge(s_two, half + 1)
                    nc.gpsimd.affine_select(out=two[:], in_=two[:], compare_op=ALU.not_equal, fill=1.0,
                                            base=-D * half, pattern=[[-1, D]], channel_multiplier=1).then_inc(s_two, 1)
                pool.wait_ge(s_two, 3)
                make_not_diag(nc, pool, v)
                with pool.Fori(0, GROUPS) as grp:
                    pool.wait_ge(s_var, grp + 1)
                    nc.gpsimd.tensor_tensor(out=lsum[:, 3, :], in0=lsum[:, 2, :], in1=power[:, 0:LNG],
                                            op=ALU.pow).then_inc(s_rstd, 1)

            @block.scalar
            def _(act):
                act.dma_start(wstage[0:D, 0, :], v["w_gat"]).then_inc(s_w, 16)
                for dup in range(2):
                    for m in range(2):
                        act.dma_start(wstage[0:D, 2 + 6 * m + dup:2 + 6 * m + 6:2, :],
                                      v["w_ih_e"].rearrange(gate_view, t=3)[:, :, D * m:D * m + D]).then_inc(s_w, 16)
                act.dma_start(wstage[0:D, 14:20:2, :], v["w_hh_e"].rearrange(gate_view, t=3)).then_inc(s_w, 16)
                act.dma_start(wstage[0:D, 15:20:2, :], v["w_hh_n"].rearrange(gate_view, t=3)).then_inc(s_w, 16)
                act.dma_start(wstage[0:D, 20:23, :], v["w_ih_n"].rearrange(gate_view, t=3)).then_inc(s_w, 16)
                with nc.allow_non_contiguous_dma(reason="a few hundred floats, once"):
                    act.dma_start(a12[:, :], v["a_gat"].rearrange("(m d) o -> d (m o)", m=2)).then_inc(s_w, 16)
                    for half, (ih, hh) in enumerate(((v["b_ih_e"], v["b_hh_e"]), (v["b_ih_n"], v["b_hh_n"]))):
                        for which, b in enumerate((ih, hh)):
                            act.dma_start(bias[D * half:D * half + D, which, :],
                                          b.rearrange("(t n) -> n t", t=3)).then_inc(s_w, 16)
                with act.Fori(0, XG // 4) as four:
                    for i in range(4):
                        act.wait_ge(s_xt, four * 4 + (i + 1))
                        nc.scalar.copy(blocks(high2, four * 16 + 4 * i), banked(i)).then_inc(s_hi, 1)
                act.wait_ge(s_wt, 1)
                nc.scalar.copy(wT[:, 0, :], ps[0:D, 1, 0, 0:D]).then_inc(s_wk, 1)
                nc.scalar.copy(wT[:, 1, :], ps[0:D, 1, 0, 0:D]).then_inc(s_wk, 1)
                nc.scalar.copy(wie[:, :, :, :].rearrange("p m t d -> p (m t d)"),
                               ps[:, 1, 1, 0:6 * D]).then_inc(s_wk, 1)
                nc.scalar.copy(whh[:, :, :].rearrange("p t (e d) -> p (t e) d", e=2),
                               ps[0:D, 1, 2, 0:6 * D].rearrange("p (t d) -> p t d", d=D)).then_inc(s_wk, 1)
                nc.scalar.copy(wihn[:, :, :], ps[0:D, 1, 0, D:4 * D].rearrange("p (t d) -> p t d", d=D)
                               ).then_inc(s_wk, 1)
                act.wait_ge(s_wp, 1)
                nc.scalar.copy(va[:, 0, :], ps[:, 1, 3, 0:2]).then_inc(s_wk, 1)
                nc.scalar.copy(va[:, 1, 0:1], ps[:, 1, 3, 1:2]).then_inc(s_wk, 1)
                nc.scalar.copy(va[:, 1, 1:2], ps[:, 1, 3, 0:1]).then_inc(s_wk, 1)
                nc.scalar.copy(w2[D:P, :, :], ps[D:P, 1, 3, D:4 * D].rearrange("p (t d) -> p t d", d=D)
                               ).then_inc(s_wk, 1)
                act.wait_ge(s_wk, 9)
                w_edge, w_node = v["w_edge"], v["w_node"]
                nc.scalar.copy(w_edge[0:D, :, :], wie[0:D, 0, 0:2, :]).then_inc(s_wk, 1)
                nc.scalar.copy(w_edge[D:P, :, :], whh[:, 0:2, 0:D]).then_inc(s_wk, 1)
                nc.scalar.copy(w_node[0:D, :, :], whh[:, 0:2, D:2 * D]).then_inc(s_wk, 1)
                nc.scalar.copy(w_node[D:P, :, :], w2[D:P, 0:2, :]).then_inc(s_wk, 1)

                def split_h(grp):
                    at = bass.ds(grp * LNG, LNG)
                    act.wait_ge(s_ln, grp + 1)
                    nc.scalar.copy(parts[:, at, 0, :], h[:, at, 1:]).then_inc(s_h0, 1)
                    for g in range(G):
                        act.dma_start(scratch[bass.ds(GQ * g + grp * (Q * LNG), Q * LNG), :].rearrange(
                            "(c jj) d -> jj c d", jj=Q), h[Q * g:Q * g + Q, bass.ds(grp * LNG, LNG), :]
                        ).then_inc(s_scr, 16)

                def make_pair(tile, t):
                    act.wait_ge(s_pair_free, tile + 1)
                    cols = bass.ds(tile * Q, Q)
                    for part, src in ((0, high2), (1, low2)):
                        half = slice(D * part, D * part + D)
                        nc.scalar.copy(pair[half, t % 2, :].rearrange("p (g q) -> p g q", g=G),
                                       src[half, :].bitcast(F32).rearrange("p (g m) -> p g m", g=G)[:, :, cols]
                                       ).then_inc(s_pair, 1)

                assert TPB % 2 == 0
                act.wait_ge(s_hi, XG)
                act.wait_ge(s_low, XG)
                with act.Fori(0, GROUPS) as grp:
                    with act.Fori(0, BODIES) as body:
                        for slot in range(RING):
                            if slot % SPT == 0:
                                make_pair(grp * LNG + body * TPB + slot // SPT, slot // SPT)
                            act.wait_ge(s_strip[slot], (grp * BODIES + body + 1) * (16 * G))
                            act.wait_ge(s_sign_free, grp * (BODIES * RING) + body * RING + slot + 1)
                            unit = grp * (LNG * SPT) + body * RING + slot
                            nc.scalar.activation(
                                signs[:, :], ring[:, slot, :], ACT.Sign,
                                accum_out=rowsign[:, :, :].rearrange("p c s -> p (c s)")[:, bass.ds(unit, 1)]
                            ).then_inc(s_sign, 1)
                            act.wait_ge(s_sign, grp * (BODIES * RING) + body * RING + slot + 1)
                            act.sem_inc(s_sign_free, 1)
                    split_h(grp)

            @block.tensor
            def _(pe):
                pe.wait_ge(s_id, 2)
                pe.wait_ge(s_x, 16 * G)
                for q in range(XG):
                    if q >= 4:
                        pe.wait_ge(s_low, q - 3)
                    for b in range(4):
                        for half in range(2):
                            last = nc.tensor.matmul(ps[D * half:D * half + D, 0, q % 4, P * b:P * b + P],
                                                    h[:, 4 * q + b, 1:], ident[:], start=True, stop=True,
                                                    skip_group_check=True)
                    last.then_inc(s_xt, 1)
                pe.wait_ge(s_w, 16 * 13)
                id64 = ident[0:D, 0:D]
                nc.tensor.transpose(ps[0:D, 1, 0, 0:D], wstage[0:D, 0, :], id64)
                for t in range(3):
                    nc.tensor.transpose(ps[0:D, 1, 0, D * (t + 1):D * (t + 2)], wstage[0:D, 20 + t, :], id64)
                for m in range(2):
                    for t in range(3):
                        o = 3 * m + t
                        nc.tensor.transpose(ps[:, 1, 1, D * o:D * o + D],
                                            wstage[0:D, 2 + 2 * o:4 + 2 * o, :].rearrange("p a d -> p (a d)"), id64)
                for o in range(6):
                    last = nc.tensor.transpose(ps[0:D, 1, 2, D * o:D * o + D], wstage[0:D, 14 + o, :], id64)
                last.then_inc(s_wt, 1)
                pe.wait_ge(s_wk, 5)
                nc.tensor.matmul(ps[:, 1, 3, 0:2], wT[:, :, :].rearrange("p a d -> p (a d)"), a12[:, :],
                                 start=True, stop=True)
                nc.tensor.matmul(ps[D:P, 1, 3, D:4 * D], wT[:, 0, :], wihn[:, :, :].rearrange("p t d -> p (t d)"),
                                 start=True, stop=True, skip_group_check=True).then_inc(s_wp, 1)
                pe.sem_inc(s_pair_free, 2)
                pe.wait_ge(s_low, XG)
                pe.wait_ge(s_wk, 13)
                with pe.Fori(0, C // TPB) as body:
                    for t in range(TPB):
                        pe.wait_ge(s_pair, (body * TPB + t) * 2 + 2)
                        for s in range(SPT):
                            strip = t * SPT + s
                            pe.wait_ge(s_gram_free, body * RING + strip + 1)
                            for b in range(4):
                                cols = slice(STRIP * s + BANK * b, STRIP * s + BANK * (b + 1))
                                o = ps[:, strip % 2, b, :]
                                nc.tensor.matmul(o, pair[:, t % 2, :], high2[:, cols], start=True, stop=False)
                                last = nc.tensor.matmul(o, pair[:, t % 2, :], low2[:, cols], start=False, stop=True)
                            last.then_inc(s_gram, 1)
                        pe.wait_ge(s_gram, body * RING + (t + 1) * SPT)
                        pe.sem_inc(s_pair_free, 1)

            @block.vector
            def _(dve):
                dve.sem_inc(s_gram_free, 2)
                dve.sem_inc(s_sign_free, 1)
                with dve.Fori(0, XG // 4) as four:
                    for i in range(4):
                        dve.wait_ge(s_hi, four * 4 + (i + 1))
                        nc.vector.tensor_tensor(out=blocks(low2, four * 16 + 4 * i), in0=banked(i),
                                                in1=blocks(high2, four * 16 + 4 * i).bitcast(F32),
                                                op=ALU.subtract).then_inc(s_low, 1)
                dve.wait_ge(s_w, 16 * 13)
                nc.vector.tensor_tensor(out=brz[:, :], in0=bias[:, 0, 0:2], in1=bias[:, 1, 0:2],
                                        op=ALU.add).then_inc(s_bias, 1)
                nc.vector.tensor_scalar(out=bhn[:, :], in0=bias[:, 1, 2:3], scalar1=0.5, scalar2=None,
                                        op0=ALU.mult).then_inc(s_bias, 1)
                dve.wait_ge(s_bias, 2)
                nc.vector.tensor_scalar(out=brz[:, :], in0=brz[:, :], scalar1=0.5, scalar2=None,
                                        op0=ALU.mult).then_inc(s_bias, 1)

                LN_STEPS = 8

                def norm(grp):
                    chain = Chain(dve, s_c, grp * LN_STEPS)
                    at = bass.ds(grp * LNG, LNG)
                    hg, wide = h[:, at, 1:], [P, LNG, D]
                    dve.wait_ge(s_gram_free, 2 + (grp + 1) * (LNG * SPT))
                    nc_sum = lsum[:, 0, :]
                    chain.after(nc.vector.tensor_reduce(nc_sum, outer[:, at, :], AX, ALU.add))
                    dve.wait_ge(s_sign, (grp + 1) * (LNG * SPT))
                    chain.after(nc.vector.tensor_reduce(h[:, at, 0], rowsign[:, at, :], AX, ALU.add))
                    chain.after(nc.vector.tensor_scalar(lsum[:, 1, :], nc_sum, -R_CONST, F_CONST, ALU.mult, ALU.add))
                    chain.after(nc.vector.scalar_tensor_tensor(
                        out=sq[:, :, :], in0=hg, scalar=1.0 - B_CONST, in1=lsum[:, 1, :].unsqueeze(2).to_broadcast(wide),
                        op0=ALU.mult, op1=ALU.add))
                    chain.after(nc.vector.tensor_reduce(nc_sum, sq[:, :, :], AX, ALU.add))
                    chain.after(nc.vector.tensor_scalar(lsum[:, 1, :], nc_sum, 1.0 / D, None, ALU.mult))
                    chain.after(nc.vector.tensor_tensor(
                        out=hg, in0=sq[:, :, :], in1=lsum[:, 1, :].unsqueeze(2).to_broadcast(wide), op=ALU.subtract))
                    chain.after(nc.vector.tensor_tensor(out=sq[:, :, :], in0=hg, in1=hg, op=ALU.mult))
                    assert chain.n == LN_STEPS
                    nc.vector.tensor_reduce(nc_sum, sq[:, :, :], AX, ALU.add).then_inc(s_h1x, 1)
                    dve.wait_ge(s_h1x, grp + 1)
                    nc.vector.tensor_scalar(lsum[:, 2, :], nc_sum, 1.0 / D, EPS, ALU.mult, ALU.add).then_inc(s_var, 1)
                    dve.wait_ge(s_rstd, grp + 1)
                    nc.vector.tensor_tensor(out=hg, in0=hg, in1=lsum[:, 3, :].unsqueeze(2).to_broadcast(wide),
                                            op=ALU.mult).then_inc(s_ln, 1)
                    dve.wait_ge(s_h0, grp + 1)
                    nc.vector.tensor_tensor(out=parts[:, at, 1, :], in0=hg, in1=parts[:, at, 0, :].bitcast(F32),
                                            op=ALU.subtract).then_inc(s_h1, 1)

                s_h1x = sem("square_sum")
                flat = outer[:, :, :].rearrange("p c s -> p (c s)")
                with dve.Fori(0, GROUPS) as grp:
                    with dve.Fori(0, BODIES) as body:
                        for slot in range(RING):
                            unit = grp * (LNG * SPT) + body * RING + slot
                            dve.wait_ge(s_strip[slot], (grp * BODIES + body + 1) * (16 * G))
                            dve.wait_ge(s_gram, unit + 1)
                            dve.wait_ge(s_gram_free, unit + 2)
                            nc.vector.scalar_tensor_tensor(
                                out=weighed[:, :], in0=ring[:, slot, :], scalar=1.0,
                                in1=ps[:, slot % 2, :, :].rearrange("p b n -> p (b n)"), op0=ALU.mult, op1=ALU.mult,
                                accum_out=flat[:, bass.ds(unit, 1)]).then_inc(s_gram_free, 1)
                    norm(grp)
                dve.wait_ge(s_h1, GROUPS)


def layer1(nc, v):
    (N, K, adj, ident, flag, dnat) = (v[k] for k in "N K adj ident flag dnat".split())
    with ExitStack() as ctx:
        def sb(name, shape, dt):
            return ctx.enter_context(nc.sbuf_tensor(name, shape, dt))

        b = dict(v)
        b["at"] = sb("at", [P, 4, v["HC"], BANK], F32)
        b["mask"] = sb("mask", [P, 2, v["HC"], BANK], F32R)
        b["nat"] = sb("nat", [P, 4, D], F32)
        b["stage"] = sb("stage", [P, 4, 1 + D], F32)
        b["hT"] = sb("hT", [P, BANK], F32)
        b["sums"] = sb("sums", [P, 2, BANK], F32)
        b["wsum"] = sb("wsum", [P, 2, BANK], F32)
        b["tr"] = sb("tr", [P, BANK], F32)
        b["tz"] = sb("tz", [P, BANK], F32)
        b["hn"] = sb("hn", [P, BANK], F32)
        b["nn"] = sb("nn", [P, BANK], F32)
        b["en"] = sb("en", [P, 4, 4], F32)
        b["co"] = sb("co", [P, 8, 4, 3], F32)
        b["prob"] = sb("prob", [P, 2, 4, D], F32)
        b["cnt"] = [b["tr"], b["tz"]]
        b["lows"] = b["nn"]
        b["seen"] = sb("seen", [P, K * v["H"]], F32)
        b["seen_k"] = sb("seen_k", [P, K], F32)
        b["pcount"] = sb("pcount", [P, K, 4], F32)
        b["dsign"] = sb("dsign", [P, K, 4], F32)
        b["seen4"] = sb("seen4", [P, K], F32)
        b["miss"] = sb("miss", [1, K + 1], F32)
        b["y"] = sb("y", [P, 4, D], F32)
        b["ysq"] = sb("ysq", [P, 4, D], F32)
        b["yo"] = sb("yo", [P, 4, D], F32)
        b["ls"] = sb("ls", [P, 4, 4], F32)
        b["s_dsign"] = v["sem"]("diagonal_signs")
        b["ps"] = ctx.enter_context(nc.psum_tensor("ps1", [P, 8, BANK], F32))
        fast = Sweep(nc, b, "f_", 1)
        full = Sweep(nc, b, "g_", 2)
        b["s_miss"], b["s_missed"], b["s_flag"] = v["sem"]("misses_by_row"), v["sem"]("misses"), v["sem"]("flag_made")
        with nc.Block() as block:
            @block.sync
            def _(sp):
                fast.sync(sp)

            @block.gpsimd
            def _(pool):
                fast.gpsimd(pool)

            @block.scalar
            def _(act):
                fast.scalar(act)

            @block.tensor
            def _(pe):
                fast.tensor(pe)
                pe.wait_ge(b["s_miss"], 4)
                nc.tensor.matmul(b["ps"][0:1, HN, 0:K], b["one"][:, :], b["seen_k"][:, :], start=True,
                                 stop=True).then_inc(b["s_missed"], 1)

            @block.vector
            def _(dve):
                fast.vector(dve)
                compare(nc, dve, b, fast)

        with nc.Block() as block:
            @block.sync
            def _(sp):
                with sp.If(sp.value_load(flag[0:1, 0:1], min_val=0, max_val=1) > 0):
                    full.sync(sp)

            @block.gpsimd
            def _(pool):
                with pool.If(pool.value_load(flag[0:1, 0:1], min_val=0, max_val=1) > 0):
                    full.gpsimd(pool)

            @block.scalar
            def _(act):
                with act.If(act.value_load(flag[0:1, 0:1], min_val=0, max_val=1) > 0):
                    full.scalar(act)

            @block.tensor
            def _(pe):
                with pe.If(pe.value_load(flag[0:1, 0:1], min_val=0, max_val=1) > 0):
                    full.tensor(pe)

            @block.vector
            def _(dve):
                with dve.If(dve.value_load(flag[0:1, 0:1], min_val=0, max_val=1) > 0):
                    full.vector(dve)


def compare(nc, dve, b, fast):
    K, s_miss = b["K"], b["s_miss"]
    assert BANK * b["N"] < 1 << 24
    dve.wait_ge(fast.s["mask_ready"], K * b["H"])
    nc.vector.tensor_reduce(b["seen_k"][:, :], b["seen"][:, :].rearrange("p (k h) -> p k h", k=K), AX,
                            ALU.add).then_inc(s_miss, 1)
    nc.vector.tensor_reduce(b["seen4"][:, :], b["pcount"][:, :, :], AX, ALU.add).then_inc(s_miss, 1)
    dve.wait_ge(s_miss, 2)
    nc.vector.tensor_tensor(out=b["seen_k"][:, :], in0=b["seen_k"][:, :], in1=b["seen4"][:, :],
                            op=ALU.subtract).then_inc(s_miss, 1)
    dve.wait_ge(s_miss, 3)
    dve.sem_inc(s_miss, 1)
    dve.wait_ge(b["s_missed"], 1)
    nc.vector.tensor_scalar(b["miss"][:, 0:K], b["ps"][0:1, HN, 0:K], 0.0, None, ALU.not_equal).then_inc(s_miss, 1)
    dve.wait_ge(s_miss, 5)
    nc.vector.tensor_reduce(b["miss"][:, K:K + 1], b["miss"][:, 0:K], AX, ALU.max).then_inc(s_miss, 1)
    dve.wait_ge(s_miss, 6)
    nc.vector.tensor_copy(b["flag"][:, :], b["miss"][:, K:K + 1]).then_inc(b["s_flag"], 1)
    dve.wait_ge(b["s_flag"], 1)


def make_not_diag(nc, pool, b):
    U = b["U"] // 2
    nc.gpsimd.memset(b["not_diag"][:], 1.0).then_inc(b["s_nd"], 1)
    for g in range(G):
        pool.wait_ge(b["s_nd"], g + 1)
        nd = b["not_diag"][Q * g:Q * g + Q, bass.DynSlice(g * U * U, U, step=U + 1), :]
        nc.gpsimd.affine_select(out=nd, in_=nd, compare_op=ALU.not_equal, fill=0.0, base=0,
                                pattern=[[0, U], [-1, Q]], channel_multiplier=1).then_inc(b["s_nd"], 1)
    pool.wait_ge(b["s_nd"], G + 1)


ACC_T, ACC_S, ACC_C = 0, 1, 2
R, Z, IN, HN, MISC = 3, 4, 5, 6, 7


class Sweep:

    SEMS = ("diag turned split mask_ready t_done s_done tlow_copied slow_copied cnt_copied "
            "s_evac t_evac summed counts small ekb expd expa kbb scaled ht_ps ht_ready gates tr tz hn g2 nn u "
            "back y_read var rstd yout stored nat_in nat_free stage_in stage_free chain")

    def __init__(self, nc, b, prefix, signs):
        self.nc, self.b, self.signs, self.prefix = nc, b, signs, prefix
        self.s = {n: b["sem"](prefix + n) for n in self.SEMS.split()}
        self.N, self.K, self.U, self.H = b["N"], b["K"], b["U"], b["H"]
        self.GQ = b["GQ"]

    def where(self, position):
        return min(position, self.H)

    def products_done(self, k):
        return (k + 1) * (self.H * self.signs) + (self.signs - 1)

    def sync(self, sp):
        b, s, U, prefix = self.b, self.s, self.U, self.prefix
        slots = b["SLOTS"]
        for u in range(U):
            if u >= slots:
                sp.wait_ge(s["turned"], 2 * (u + 1 - slots))
            if self.signs == 2 or u >= slots:
                load_unit(sp, b, prefix, 0, u)
        with sp.Fori(1, self.K) as k:
            for u in range(U):
                sp.wait_ge(s["turned"], k * (2 * U) + 2 * (u + 1 - slots))
                load_unit(sp, b, prefix, k, u)

    def gpsimd(self, pool):
        nc, b, s = self.nc, self.b, self.s
        U, RB, UC, K, SLOTS = self.U, b["RB"], b["UC"], self.K, b["SLOTS"]

        def no_diagonal(k):
            for u in range(U):
                raw = unit_view(b, u % SLOTS)[:, (u % 2) * UC * (UC * Q):(u % 2 + 1) * UC * (UC * Q)]
                diag = bass.AP(tensor=raw.tensor, offset=raw.offset,
                               ap=[list(raw.ap[0]), [UC * Q + Q, UC], [1, Q]])
                pool.wait_ge(b["s_raw"][self.prefix][u % SLOTS], (k * (U // SLOTS) + u // SLOTS + 1) * (16 * G))
                carry(pool, b["s_carry"])
                nc.gpsimd.tensor_tensor(
                    out=diag, in0=diag,
                    in1=b["not_diag"][:, bass.ds(k * (U // 2) + u // 2, 1), :].to_broadcast([P, UC, Q]),
                    op=ALU.mult).then_inc(s["diag"], 1)

        def end(k):
            pool.wait_ge(s["var"], k + 1)
            nc.gpsimd.tensor_tensor(out=b["ls"][:, 3, :], in0=b["ls"][:, 2, :], in1=b["power"][:, 0:4],
                                    op=ALU.pow).then_inc(s["rstd"], 1)

        if self.signs == 2:
            with pool.Fori(0, K) as k:
                no_diagonal(k)
                end(k)
        else:
            no_diagonal(0)
            with pool.Fori(1, K) as k:
                no_diagonal(k)
                end(k - 1)
            end(K - 1)

    def vector(self, dve):
        nc, b, s, ps = self.nc, self.b, self.s, self.b["ps"]
        H, HC, RB, UC, K, N, signs = self.H, b["HC"], b["RB"], b["UC"], self.K, self.N, self.signs
        hi = slice(D, P)

        def turn(k, half, first):
            n = k * H + half
            u, part = half // 2, half % 2
            if part == 0:
                dve.wait_ge(s["diag"], k * self.U + u + 1)
            slot = half % 4 if signs == 1 else 0
            if signs == 1:
                if not (first and half < 4):
                    dve.wait_ge(s["t_done"], n - 3)
                    dve.wait_ge(s["mask_ready"], n - 3)
            raw = unit_view(b, u % b["SLOTS"]).rearrange("p (f c q) -> p f c q", f=RB, q=Q)
            nc.vector.transpose(
                b["at"][:, slot, :, :].rearrange("p c (f q) -> p f c q", q=Q),
                raw[:, :, HC * part:HC * part + HC, :]).then_inc(s["turned"], 1)
            if signs == 2:
                dve.wait_ge(s["turned"], n + 1)
                for i, sign in enumerate((1.0, -1.0)):
                    m = n * 2 + i
                    dve.wait_ge(s["s_done"], m + 1)
                    dve.wait_ge(s["t_done"], m + 1)
                    nc.vector.tensor_scalar(b["at"][:, 1, :, :], b["at"][:, 0, :, :], sign, 0.0,
                                            ALU.mult, ALU.max).then_inc(s["split"], 1)
                    nc.vector.tensor_scalar(b["mask"][:, 0, :, :], b["at"][:, 0, :, :], sign, 0.0,
                                            ALU.mult, ALU.is_gt).then_inc(s["mask_ready"], 1)
                    dve.wait_ge(s["split"], m + 1)
                    dve.wait_ge(s["mask_ready"], m + 1)

        CHAIN = {1: 23, 2: 32}[signs]

        def evac(k, c):
            dve.wait_ge(s["s_done"], self.products_done(k))
            for i in range(signs):
                wsum, sums = b["wsum"][hi, i, :], b["sums"][0:D, i, :]
                nc.vector.tensor_copy(wsum, ps[hi, 3 * i + ACC_T, :]).then_inc(s["t_evac"], 1)
                nc.vector.tensor_copy(sums, ps[0:D, 3 * i + ACC_S, :]).then_inc(s["s_evac"], 1)
                dve.wait_ge(s["t_evac"], k * signs + i + 1)
                dve.wait_ge(s["tlow_copied"], k * signs + i + 1)
                c.after(nc.vector.tensor_tensor(out=wsum, in0=wsum, in1=b["lows"][hi, :], op=ALU.add))
                dve.wait_ge(s["s_evac"], k * signs + i + 1)
                dve.wait_ge(s["slow_copied"], k * signs + i + 1)
                nc.vector.tensor_tensor(out=sums, in0=sums, in1=b["lows"][0:D, :], op=ALU.add).then_inc(s["summed"], 1)

        def counts(k, c):
            dve.wait_ge(s["stage_in"], k * 16 + 16)
            carry(dve, b["s_carry"])
            nc.vector.tensor_tensor(out=b["pcount"][:, bass.ds(k, 1), :].rearrange("p k e -> p (k e)"),
                                    in0=b["stage"][:, :, 0],
                                    in1=b["dsign"][:, bass.ds(k, 1), :].rearrange("p k e -> p (k e)"),
                                    op=ALU.subtract).then_inc(s["counts"], 1)
            dve.wait_ge(s["counts"], k + 2)

        def softmax(k, c):
            en, co = b["en"], b["co"]
            logit, count = en[:, :, 0:signs], en[:, :, 2:2 + signs]
            if signs == 1:
                count = b["pcount"][:, bass.ds(k, 1), :].rearrange("p k e -> p (k e)").unsqueeze(2)
            col = lambda j, w=signs: co[:, j, :, 0:w]
            dve.wait_ge(s["small"], k + 1)
            for part in (0, 2)[0:signs]:
                c.after(nc.vector.tensor_copy(
                    en[:, :, part:part + signs],
                    ps[:, HN, 0:16].rearrange("p (b e) -> p b e", b=4)[:, :, part:part + signs]))
            c.after(nc.vector.scalar_tensor_tensor(out=col(0), in0=logit, scalar=ALPHA, in1=logit,
                                                   op0=ALU.mult, op1=ALU.max))
            c.after(nc.vector.tensor_scalar(col(1), count, 0.0, None, ALU.is_gt))
            c.after(nc.vector.tensor_tensor(out=col(0), in0=col(0), in1=col(1), op=ALU.mult))
            c.after(nc.vector.tensor_scalar(col(1), col(1), -1.0, -NEG_INF, ALU.add, ALU.mult))
            c.after(nc.vector.tensor_tensor(out=col(0), in0=col(0), in1=col(1), op=ALU.add))
            if signs == 2:
                c.after(nc.vector.tensor_tensor(out=co[:, 2, :, 0], in0=co[:, 0, :, 0], in1=co[:, 0, :, 1],
                                                op=ALU.max))
                c.after(nc.vector.tensor_scalar(co[:, 2, :, 0], co[:, 2, :, 0], NEG_INF, None, ALU.max))
            else:
                c.after(nc.vector.tensor_scalar(co[:, 2, :, 0], co[:, 0, :, 0], NEG_INF, None, ALU.max))
            for i in range(signs):
                c.after(nc.vector.tensor_tensor(out=co[:, 3, :, i], in0=co[:, 0, :, i], in1=co[:, 2, :, 0],
                                                op=ALU.subtract))
            nc.vector.tensor_scalar(co[:, 3, :, signs], co[:, 2, :, 0], -1.0, NEG_INF, ALU.mult,
                                    ALU.add).then_inc(s["expa"], 1)
            if signs == 2:
                c.after(nc.vector.tensor_tensor(out=co[:, 5, :, 0], in0=en[:, :, 2], in1=en[:, :, 3], op=ALU.add))
                c.after(nc.vector.tensor_scalar(co[:, 5, :, 2], co[:, 5, :, 0], -1.0, float(N), ALU.mult, ALU.add))
            else:
                c.after(nc.vector.tensor_scalar(co[:, 5, :, 2:3], count, -1.0, float(N), ALU.mult, ALU.add))

        def probabilities(k, c):
            en, co = b["en"], b["co"]
            zeros = co[:, 5, :, 2]
            count = en[:, :, 2:2 + signs]
            if signs == 1:
                count = b["pcount"][:, bass.ds(k, 1), :].rearrange("p k e -> p (k e)").unsqueeze(2)
            dve.wait_ge(s["expd"], k + 1)
            c.after(nc.vector.tensor_tensor(out=co[:, 6, :, 0:signs], in0=co[:, 4, :, 0:signs], in1=count,
                                            op=ALU.mult))
            c.after(nc.vector.tensor_tensor(out=co[:, 6, :, 2], in0=co[:, 4, :, signs], in1=zeros, op=ALU.mult))
            for i in range(signs):
                c.after(nc.vector.tensor_tensor(out=co[:, 6, :, 2], in0=co[:, 6, :, 2], in1=co[:, 6, :, i],
                                                op=ALU.add))
            c.after(nc.vector.reciprocal(co[:, 7, :, 0], co[:, 6, :, 2]))
            for i in range(signs):
                c.after(nc.vector.tensor_tensor(out=co[:, 7, :, 1 + i], in0=co[:, 4, :, i], in1=co[:, 7, :, 0],
                                                op=ALU.mult))
                nc.vector.tensor_copy(b["prob"][:, i, :, :],
                                      co[:, 7, :, 1 + i:2 + i].to_broadcast([P, 4, D])).then_inc(s["ekb"], 1)

        def scale(k, c):
            dve.wait_ge(s["kbb"], k + 1)
            if signs == 2:
                c.after(nc.vector.tensor_tensor(out=b["wsum"][hi, 1, :], in0=ps[hi, R, :], in1=b["wsum"][hi, 1, :],
                                                op=ALU.mult))
                c.after(nc.vector.tensor_tensor(out=b["wsum"][hi, 0, :], in0=ps[hi, IN, :], in1=b["wsum"][hi, 0, :],
                                                op=ALU.mult))
                nc.vector.tensor_tensor(out=b["wsum"][hi, 0, :], in0=b["wsum"][hi, 0, :], in1=b["wsum"][hi, 1, :],
                                        op=ALU.subtract).then_inc(s["scaled"], 1)
            else:
                nc.vector.tensor_tensor(out=b["wsum"][hi, 0, :], in0=ps[hi, IN, :], in1=b["wsum"][hi, 0, :],
                                        op=ALU.mult).then_inc(s["scaled"], 1)

        def reset(k, c):
            dve.wait_ge(s["tr"], k + 1)
            dve.wait_ge(s["hn"], k + 1)
            dve.wait_ge(s["gates"], k * 3 + 2)
            c.after(nc.vector.scalar_tensor_tensor(out=b["hn"][:, :], in0=b["tr"][:, :], scalar=1.0,
                                                   in1=b["hn"][:, :], op0=ALU.add, op1=ALU.mult))
            nc.vector.tensor_tensor(out=b["hn"][:, :], in0=ps[:, IN, :], in1=b["hn"][:, :],
                                    op=ALU.add).then_inc(s["g2"], 1)

        def update(k, c):
            dve.wait_ge(s["nn"], k + 1)
            dve.wait_ge(s["ht_ready"], (k + 1) * 3)
            dve.wait_ge(s["tz"], k + 1)
            c.after(nc.vector.tensor_tensor(out=b["hT"][:, :], in0=b["hT"][:, :], in1=b["nn"][:, :],
                                            op=ALU.subtract))
            c.after(nc.vector.scalar_tensor_tensor(out=b["tz"][:, :], in0=b["tz"][:, :], scalar=1.0,
                                                   in1=b["hT"][:, :], op0=ALU.add, op1=ALU.mult))
            nc.vector.scalar_tensor_tensor(out=b["hT"][:, :], in0=b["tz"][:, :], scalar=0.5, in1=b["nn"][:, :],
                                           op0=ALU.mult, op1=ALU.add).then_inc(s["u"], 1)

        def norm(k, c):
            y, ls, wide = b["y"], b["ls"], [P, 4, D]
            dve.wait_ge(s["back"], k + 1)
            dve.wait_ge(s["nat_in"], k * 16 + 16)
            nc.vector.tensor_tensor(
                out=y[:, :, :], in0=ps[:, MISC, 0:4 * D].rearrange("p (b d) -> p b d", d=D),
                in1=b["dnat"][:, bass.ds(k * 4, 4)].unsqueeze(2).to_broadcast(wide), op=ALU.mult).then_inc(s["y_read"], 1)
            dve.wait_ge(s["y_read"], k + 2)
            nc.vector.tensor_tensor(out=y[:, :, :], in0=y[:, :, :], in1=b["nat"][:, :, :],
                                    op=ALU.add).then_inc(s["nat_free"], 1)
            dve.wait_ge(s["nat_free"], k + 2)
            c.after(nc.vector.tensor_reduce(ls[:, 0, :], y[:, :, :], AX, ALU.add))
            c.after(nc.vector.tensor_scalar(ls[:, 1, :], ls[:, 0, :], 1.0 / D, None, ALU.mult))
            c.after(nc.vector.tensor_tensor(out=y[:, :, :], in0=y[:, :, :],
                                            in1=ls[:, 1, :].unsqueeze(2).to_broadcast(wide), op=ALU.subtract))
            c.after(nc.vector.tensor_tensor(out=b["ysq"][:, :, :], in0=y[:, :, :], in1=y[:, :, :], op=ALU.mult))
            c.after(nc.vector.tensor_reduce(ls[:, 0, :], b["ysq"][:, :, :], AX, ALU.add))
            nc.vector.tensor_scalar(ls[:, 2, :], ls[:, 0, :], 1.0 / D, EPS, ALU.mult, ALU.add).then_inc(s["var"], 1)

        def result(k, c):
            dve.wait_ge(s["rstd"], k + 1)
            dve.wait_ge(s["stored"], k * 16 + 16)
            nc.vector.tensor_tensor(out=b["yo"][:, :, :], in0=b["y"][:, :, :],
                                    in1=b["ls"][:, 3, :].unsqueeze(2).to_broadcast([P, 4, D]),
                                    op=ALU.mult).then_inc(s["yout"], 1)

        if signs == 1:
            dve.wait_ge(b["s_dsign"], 1)
            dve.sem_inc(s["counts"], 1)
        dve.sem_inc(s["y_read"], 1)
        dve.sem_inc(s["nat_free"], 1)
        dve.sem_inc(s["stored"], 16)
        steps = ((counts, 1), (evac, 2), (softmax, 5), (probabilities, 6), (scale, 8), (reset, 10), (update, 12),
                 (norm, 14), (result, 16))
        if signs == 2:
            steps = steps[1:]
        self.weave(dve, turn, steps, CHAIN)

    def weave(self, eng, half_step, steps, chain_length=None):
        def run(k, first, prev):
            chain = None if prev is None or chain_length is None else Chain(eng, self.s["chain"], prev * chain_length)

            def at(position):
                for step, where in steps:
                    if prev is not None and self.where(where) == position:
                        step(prev, chain)

            for half in range(self.H):
                at(half)
                if k is not None:
                    half_step(k, half, first)
            at(self.H)
            if chain is not None and chain.n != chain_length:
                raise AssertionError(chain.n)

        if self.signs == 2:
            for k, first in ((0, True), (None, False)):
                if first:
                    run(0, True, None)
                    run(None, False, 0)
                else:
                    with eng.Fori(1, self.K) as i:
                        run(i, False, None)
                        run(None, False, i)
        else:
            run(0, True, None)
            with eng.Fori(1, self.K) as i:
                run(i, False, i - 1)
            run(None, False, self.K - 1)

    def scalar(self, act):
        nc, b, s, ps = self.nc, self.b, self.s, self.b["ps"]
        H, signs = self.H, self.signs
        hi = slice(D, P)

        def sign(k, half, first):
            if half == H // 4:
                if first:
                    act.wait_ge(b["s_scr"], 16 * G * (b["C"] // b["LNG"]))
                staged_rows(k)
            if signs == 2:
                return
            n = k * H + half
            act.wait_ge(s["turned"], n + 1)
            if not (first and half < 2):
                act.wait_ge(s["s_done"], n - 1)
            nc.scalar.activation(
                b["mask"][:, half % 2, :, :].rearrange("p c i -> p (c i)"),
                b["at"][:, half % 4, :, :].rearrange("p c i -> p (c i)").bitcast(U32), ACT.Sign,
                accum_out=b["seen"][:, bass.ds(n, 1)]).then_inc(s["mask_ready"], 1)

        def evac(k, c):
            act.wait_ge(s["s_done"], self.products_done(k))
            for i in range(signs):
                if i == 1:
                    act.wait_ge(s["summed"], k * signs + 1)
                nc.scalar.copy(b["lows"][hi, :], ps[0:D, 3 * i + ACC_T, :]).then_inc(s["tlow_copied"], 1)
                nc.scalar.copy(b["lows"][0:D, :], ps[hi, 3 * i + ACC_S, :]).then_inc(s["slow_copied"], 1)
                if signs == 2:
                    nc.scalar.copy(b["cnt"][i][0:D, :], ps[0:D, 3 * i + ACC_C, :]).then_inc(s["cnt_copied"], 1)
            act.wait_ge(s["ht_ps"], k + 1)
            nc.scalar.copy(b["hT"][:, :], ps[:, MISC, :]).then_inc(s["ht_ready"], 1)
            nc.scalar.copy(b["sums"][hi, 0, :], ps[hi, MISC, :]).then_inc(s["ht_ready"], 1)
            nc.scalar.copy(b["wsum"][0:D, 0, :], ps[0:D, MISC, :]).then_inc(s["ht_ready"], 1)

        def exps(k, c):
            act.wait_ge(s["expa"], k + 1)
            nc.scalar.activation(b["co"][:, 4, :, 0:signs + 1], b["co"][:, 3, :, 0:signs + 1],
                                 ACT.Exp).then_inc(s["expd"], 1)

        def gates(k, c):
            act.wait_ge(s["gates"], k * 3 + 1)
            nc.scalar.activation(b["tr"][:, :], ps[:, R, :], ACT.Tanh, bias=b["brz"][:, 0:1],
                                 scale=0.5).then_inc(s["tr"], 1)
            nc.scalar.activation(b["hn"][:, :], ps[:, HN, :], ACT.Identity, bias=b["bhn"][:, 0:1],
                                 scale=0.5).then_inc(s["hn"], 1)
            act.wait_ge(s["gates"], k * 3 + 3)
            nc.scalar.activation(b["tz"][:, :], ps[:, Z, :], ACT.Tanh, bias=b["brz"][:, 1:2],
                                 scale=0.5).then_inc(s["tz"], 1)

        def new(k, c):
            act.wait_ge(s["g2"], k + 1)
            nc.scalar.activation(b["nn"][:, :], b["hn"][:, :], ACT.Tanh,
                                 bias=b["bias"][:, 0, 2:3]).then_inc(s["nn"], 1)

        def rows(k, c):
            act.wait_ge(s["nat_free"], k + 1)
            act.dma_start(b["nat"][:, :, :], b["scratch"][bass.ds(k * BANK, BANK), :].rearrange(
                "(b p) d -> p b d", p=P)[:, :, 1:]).then_inc(s["nat_in"], 16)

        def staged_rows(k):
            act.wait_ge(s["stage_free"], k + 1)
            if signs == 1:
                act.wait_ge(s["counts"], k + 1)
            act.dma_start(b["stage"][:, :, :], b["scratch"][bass.ds(k * BANK, BANK), :].rearrange(
                "(b p) d -> p b d", p=P)).then_inc(s["stage_in"], 16)

        def store(k, c):
            act.wait_ge(s["yout"], k + 1)
            act.dma_start(b["out"][bass.ds(k * BANK, BANK), :].rearrange("(b p) d -> p b d", p=P),
                          b["yo"][:, :, :]).then_inc(s["stored"], 16)

        if signs == 1:
            nc.scalar.activation(b["dsign"][:, :, :].rearrange("p k e -> p (k e)"), b["dnat"][:, :],
                                 ACT.Sign).then_inc(b["s_dsign"], 1)
        self.weave(act, sign, ((rows, 1), (evac, 1), (exps, 5), (gates, 8), (new, 10), (store, 16)))
        act.wait_ge(s["stored"], 16 * (self.K + 1))

    def tensor(self, pe):
        nc, b, s, ps = self.nc, self.b, self.s, self.b["ps"]
        H, HC, signs = self.H, b["HC"], self.signs
        hi = slice(D, P)
        h, parts = b["h"], b["parts"][:, :, :, :].rearrange("p c e d -> p c (e d)")
        mm = nc.tensor.matmul

        def products(k, half, first):
            for i in range(signs):
                n = (k * H + half) * signs + i
                slot = half % 4 if signs == 1 else 1
                mslot = half % 2 if signs == 1 else 0
                if half == 0 and i == 0 and not first:
                    pe.wait_ge(s["tlow_copied"], k * signs)
                    pe.wait_ge(s["t_evac"], k * signs)
                pe.wait_ge(s["turned" if signs == 1 else "split"], n + 1)
                for cl in range(HC):
                    c = half * HC + cl
                    o = ps[D * (cl % 2):D * (cl % 2) + D, 3 * i + ACC_T, :]
                    last = mm(o, h[:, c, 1:], b["at"][:, slot, cl, :], start=c < 2, stop=c >= H * HC - 2)
                last.then_inc(s["t_done"], 1)
                if half == 0 and i == 0 and not first:
                    pe.wait_ge(s["slow_copied"], k * signs)
                    pe.wait_ge(s["s_evac"], k * signs)
                    if signs == 2:
                        pe.wait_ge(s["cnt_copied"], k * signs)
                pe.wait_ge(s["mask_ready"], n + 1)
                for cl in range(HC):
                    c = half * HC + cl
                    ends = dict(start=c == 0, stop=c == H * HC - 1)
                    last = mm(ps[:, 3 * i + ACC_S, :], parts[:, c, :], b["mask"][:, mslot, cl, :], **ends)
                    if signs == 2:
                        last = mm(ps[:, 3 * i + ACC_C, :], b["ones"][:, :], b["mask"][:, mslot, cl, :], **ends)
                last.then_inc(s["s_done"], 1)

        def turn_h(k, c):
            pe.wait_ge(s["stage_in"], k * 16 + 16)
            pe.wait_ge(s["y_read"], k + 1)
            for i in range(4):
                for half in range(2):
                    last = mm(ps[D * half:D * half + D, MISC, P * i:P * i + P], b["stage"][:, i, 1:], b["ident"][:],
                              start=True, stop=True)
            last.then_inc(s["ht_ps"], 1)
            pe.wait_ge(s["ht_ps"], k + 1)
            pe.sem_inc(s["stage_free"], 1)

        def small(k, c):
            pe.wait_ge(s["summed"], (k + 1) * signs)
            if signs == 2:
                pe.wait_ge(s["cnt_copied"], (k + 1) * signs)
            en = ps[:, HN, 0:16].rearrange("p (b e) -> p b e", b=4)
            for q in range(4):
                cols = slice(P * q, P * q + P)
                for i in range(signs):
                    last = mm(en[:, q, 0:signs], b["sums"][0:D, i, cols], b["va"][0:D, i, 0:signs],
                       start=i == 0, stop=i == signs - 1)
                if signs == 2:
                    for i in range(signs):
                        last = mm(en[:, q, 2 + i:3 + i], b["cnt"][i][0:D, cols], b["pick"][0:D, :], start=True, stop=True)
            last.then_inc(s["small"], 1)

        def spread(k, c):
            pe.wait_ge(s["ekb"], (k + 1) * signs)
            for i in range(signs):
                for q in range(4):
                    last = mm(ps[hi, (IN, R)[i], P * q:P * q + P], b["prob"][:, i, q, :], b["ident"][:, :],
                              start=True, stop=True)
            last.then_inc(s["kbb"], 1)

        def gates(k, c):
            pe.wait_ge(s["ht_ready"], (k + 1) * 3)
            sums, wsum, lo = b["sums"], b["wsum"], slice(0, D)
            mm(ps[:, HN, :], b["whh"][:, 2, :], b["hT"][0:D, :], start=True, stop=True)
            pe.wait_ge(s["scaled"], k + 1)

            def r_or_z(t, bank):
                mm(ps[lo, bank, :], b["w_edge"][:, t, :], sums[:, 0, :], start=True, stop=signs == 1)
                if signs == 2:
                    mm(ps[lo, bank, :], b["wie"][lo, 1, t, :], sums[lo, 1, :], start=False, stop=True)
                mm(ps[hi, bank, :], b["w_node"][:, t, :], wsum[:, 0, :], start=True, stop=True,
                   skip_group_check=True).then_inc(s["gates"], 1)

            r_or_z(0, R)
            for i in range(signs):
                mm(ps[lo, IN, :], b["wie"][lo, i, 2, :], sums[lo, i, :], start=i == 0, stop=i == signs - 1)
            mm(ps[hi, IN, :], b["w2"][hi, 2, :], wsum[hi, 0, :], start=True, stop=True,
               skip_group_check=True).then_inc(s["gates"], 1)
            r_or_z(1, Z)

        def back(k, c):
            pe.wait_ge(s["u"], k + 1)
            for q in range(4):
                last = mm(ps[:, MISC, D * q:D * q + D], b["hT"][:, P * q:P * q + P], b["two"][:, :],
                          start=True, stop=True)
            last.then_inc(s["back"], 1)

        pe.sem_inc(s["stage_free"], 1)
        if signs == 2:
            pe.sem_inc(s["t_done"], 1)
            pe.sem_inc(s["s_done"], 1)
        self.weave(pe, products, ((turn_h, 0), (small, 2), (spread, 5), (gates, 7), (back, 11)))


_INS = ["x", "adj", "L1_gnn_W_gat", "L1_gnn_a_gat", "L1_gnn_w_ih_e", "L1_gnn_w_hh_e", "L1_gnn_b_ih_e",
        "L1_gnn_b_hh_e", "L1_gnn_w_ih_n", "L1_gnn_w_hh_n", "L1_gnn_b_ih_n", "L1_gnn_b_hh_n"]


def kernel(**inputs):
    import numpy as _np
    import concourse.bacc as _bacc
    from concourse import mybir as _mybir
    from concourse.bass_utils import run_bass_kernel_spmd as _run

    nc = _bacc.Bacc("TRN2", target_bir_lowering=False, num_devices=1)
    arrays, args = {}, []
    for name in _INS:
        a = _np.ascontiguousarray(inputs[name])
        arrays[f"in_{name}"] = a
        args.append(nc.dram_tensor(f"in_{name}", a.shape, _mybir.dt.from_np(a.dtype), kind="ExternalInput").ap())
    shape = inputs["x"].shape
    out = nc.dram_tensor("out_0", shape, _mybir.dt.float32, kind="ExternalOutput").ap()
    build_gnn(nc, *args, out)
    return _run(nc, [arrays], core_ids=[0]).results[0]["out_0"]
```

```python
from contextlib import ExitStack

import concourse.bass as bass
from concourse import mybir

P = 128
Q = 32
G = P // Q
BANK = 512
D = 64
EPS = 1e-5
ALPHA = 0.2
NEG_INF = -9000000000000000.0
F_CONST, B_CONST, R_CONST = 1.0, 0.1, 0.01

ALU = mybir.AluOpType
ACT = mybir.ActivationFunctionType
F32 = mybir.dt.float32
BF16 = mybir.dt.bfloat16
F32R = mybir.dt.float32r
U32 = mybir.dt.uint32
I32 = mybir.dt.int32
AX = mybir.AxisListType.X


def carry(eng, s_carry):
    eng.sem_inc(s_carry, 1)


class Chain:

    def __init__(self, eng, sem, base=0):
        self.eng, self.sem, self.base, self.n = eng, sem, base, 0

    def after(self, ins):
        self.n += 1
        ins.then_inc(self.sem, 1)
        self.eng.wait_ge(self.sem, self.base + self.n)


def build_gnn(nc, x, adj, w_gat, a_gat, w_ih_e, w_hh_e, b_ih_e, b_hh_e, w_ih_n, w_hh_n, b_ih_n, b_hh_n, out):
    N = adj.shape[0]
    GQ = N // G
    C = GQ // Q
    NB = N // P
    assert N % 2048 == 0 and x.shape[1] == D

    STRIP = 4 * BANK
    SPT = N // STRIP
    RING = 8
    TPB = RING // SPT
    LNG = min(8, C)
    BODIES = LNG // TPB
    GROUPS = C // LNG
    XG = C // 4

    K = N // BANK
    UC = 8
    U = C // UC
    SLOTS = min(4, U)
    HC = UC // 2
    H = 2 * U
    RB = BANK // Q

    scratch = nc.dram_tensor("h_rows", (Q, G * C, D + 1), F32, kind="Internal").ap()
    stack = ExitStack()

    def sem(name):
        return stack.enter_context(nc.semaphore(name))

    def keep(name, shape, dt):
        return stack.enter_context(nc.sbuf_tensor(name, shape, dt))

    with stack:
        h = keep("h", [P, C, D + 1], F32)
        parts = keep("parts", [P, C, 2, D], F32R)
        ones = keep("ones", [P, P], F32R)
        one = keep("one", [P, 1], F32)
        ring = keep("ring", [P, RING, STRIP], F32)
        ident = keep("ident", [P, P], F32)
        flag = keep("flag", [1, 1], I32)
        wT = keep("wT", [D, 2, D], F32)
        a12 = keep("a12", [D, 2], F32)
        wie = keep("wie", [P, 2, 3, D], F32)
        whh = keep("whh", [D, 3, 2 * D], F32)
        w2 = keep("w2", [P, 3, D], F32)
        w_edge = keep("w_edge", [P, 2, D], F32)
        w_node = keep("w_node", [P, 2, D], F32)
        va = keep("va", [P, 2, 2], F32)
        pick = keep("pick", [P, 1], F32)
        two = keep("two", [P, D], F32)
        dnat = keep("dnat", [P, NB], F32)
        bias = keep("bias", [P, 2, 3], F32)
        brz = keep("brz", [P, 2], F32)
        bhn = keep("bhn", [P, 1], F32)
        not_diag = keep("not_diag", [P, K * U // 2, Q], F32)
        power = keep("power", [P, LNG], F32)

        s_carry = sem("carries_waits")
        s_nd = sem("not_diag_made")
        s_scr = sem("h_stored")
        s_raw = {prefix: [sem(f"{prefix}unit_loaded{i}") for i in range(SLOTS)] for prefix in ("f_", "g_")}

        v = dict(locals())
        layer0(nc, v)
        layer1(nc, v)


def load_unit(sp, v, prefix, k, u):
    RB, UC, GQ, slot = v["RB"], v["UC"], v["GQ"], u % v["SLOTS"]
    raw = unit_view(v, slot).rearrange("p (f m) -> p f m", f=RB)
    for g in range(G):
        sp.dma_start(
            raw[Q * g:Q * g + Q, :, :],
            v["adj"][bass.ds(k * BANK, BANK), GQ * g + UC * Q * u:GQ * g + UC * Q * (u + 1)].rearrange(
                "(f ii) m -> ii f m", ii=Q)).then_inc(v["s_raw"][prefix][slot], 16)


def unit_view(v, slot):
    return v["ring"][:, 2 * slot:2 * slot + 2, :].rearrange("p r m -> p (r m)")


def layer0(nc, v):
    (N, GQ, C, STRIP, SPT, RING, TPB, LNG, BODIES, GROUPS, XG) = (
        v[k] for k in "N GQ C STRIP SPT RING TPB LNG BODIES GROUPS XG".split())
    (x, adj, h, parts, ones, one, ring, ident, wT, a12, wie, whh, w2, va, pick, bias, brz, bhn,
     power, sem, scratch, two, dnat, s_carry) = (
        v[k] for k in ("x adj h parts ones one ring ident wT a12 wie whh w2 va pick bias brz bhn "
                       "power sem scratch two dnat s_carry").split())

    with ExitStack() as ctx:
        def sb(name, shape, dt):
            return ctx.enter_context(nc.sbuf_tensor(name, shape, dt))

        high2 = sb("high2", [P, N], F32R)
        low2 = sb("low2", [P, N], F32R)
        pair = sb("pair", [P, 2, P], F32R)
        weighed = sb("weighed", [P, STRIP], F32)
        wstage = weighed[:, :].rearrange("p (a d) -> p a d", d=D)
        signs = sb("signs", [P, STRIP], BF16)
        outer = sb("outer", [P, C, SPT], F32)
        rowsign = sb("rowsign", [P, C, SPT], F32)
        wihn = sb("wihn", [D, 3, D], F32)
        lsum = sb("lsum", [P, 4, LNG], F32)
        sq = weighed[:, 0:LNG * D].rearrange("p (c d) -> p c d", d=D)
        ps = ctx.enter_context(nc.psum_tensor("ps", [P, 2, 4, BANK], F32))

        s_x = [sem(f"x_loaded{i}") for i in range(4)]
        s_w = sem("weights_loaded")
        s_strip = [sem(f"strip_loaded{i}") for i in range(RING)]
        s_const = sem("constants_made")
        s_bias = sem("biases_made")
        s_id = sem("ident_made")
        s_two = sem("two_made")
        s_diag = sem("diagonal_loaded")
        s_wt = sem("weights_transposed")
        s_wk = sem("weights_kept")
        s_wp = sem("weight_products")
        s_xt = sem("xt_transposed")
        s_hi = sem("hi_ready")
        s_low = sem("low_ready")
        s_pair_free = sem("pair_free")
        s_pair = sem("pair_ready")
        s_gram = sem("gram_ready")
        s_gram_free = sem("gram_free")
        s_sign = sem("signs_summed")
        s_sign_free = sem("sign_strip_done")
        s_c = sem("vector_chain0")
        s_var = sem("variance_ready")
        s_rstd = sem("rstd_ready")
        s_ln = sem("ln_done")
        s_sqsum = sem("square_sum")
        s_h0 = sem("h_high_ready")
        s_h1 = sem("h_low_ready")
        s_scr = v["s_scr"]
        gate_view = "(t n) k -> n t k"

        def blocks(part, c):
            return part[:, :].rearrange("p (g c q) -> p c g q", g=G, q=Q)[:, bass.ds(c, 4), :, :]

        def banked(i):
            return ps[:, 0, i, :].rearrange("p (c g q) -> p c g q", c=4, g=G)

        with nc.Block() as block:
            @block.sync
            def _(sp):
                for part in range(4):
                    cs = slice(part * C // 4, (part + 1) * C // 4)
                    for g in range(G):
                        sp.dma_start(h[Q * g:Q * g + Q, cs, 1:],
                                     x[GQ * g:GQ * g + GQ, :].rearrange("(c jj) d -> jj c d", jj=Q)[:, cs, :]
                                     ).then_inc(s_x[part], 16)

                def load(tile, strip, slot):
                    for g in range(G):
                        sp.dma_start(ring[Q * g:Q * g + Q, slot, :],
                                     adj[bass.ds(Q * tile + GQ * g, Q), STRIP * strip:STRIP * (strip + 1)]
                                     ).then_inc(s_strip[slot], 16)

                for slot in range(RING):
                    load(slot // SPT, slot % SPT, slot)
                with nc.allow_non_contiguous_dma(reason="the diagonal, once"):
                    sp.dma_start(dnat[:, :], adj.rearrange("i j -> (i j)")[0:N * N:N + 1].rearrange(
                        "(b p) -> p b", p=P)).then_inc(s_diag, 16)
                with sp.Fori(1, C // TPB) as body:
                    for slot in range(RING):
                        sp.wait_ge(s_gram_free, 2 + (body - 1) * RING + slot + 1)
                        carry(sp, s_carry)
                        sp.wait_ge(s_sign, (body - 1) * RING + slot + 1)
                        carry(sp, s_carry)
                        load(body * TPB + slot // SPT, slot % SPT, slot)
                for u in range(v["SLOTS"]):
                    sp.wait_ge(s_gram_free, 2 + C * SPT - RING + 2 * (u + 1))
                    sp.wait_ge(s_sign, C * SPT - RING + 2 * (u + 1))
                    load_unit(sp, v, "f_", 0, u)
                sp.wait_ge(s_diag, 16)

            @block.gpsimd
            def _(pool):
                nc.gpsimd.memset(ident[:], 0.0).then_inc(s_id, 1)
                nc.gpsimd.memset(one[:], 1.0).then_inc(s_const, 1)
                nc.gpsimd.memset(power[:], -0.5).then_inc(s_const, 1)
                nc.gpsimd.memset(pick[:], 0.0).then_inc(s_const, 1)
                pool.wait_ge(s_id, 1)
                nc.gpsimd.affine_select(out=ident[:], in_=ident[:], compare_op=ALU.not_equal, fill=1.0,
                                        base=0, pattern=[[-1, P]], channel_multiplier=1).then_inc(s_id, 1)
                pool.wait_ge(s_id, 2)
                nc.gpsimd.tensor_scalar(ones[:, :], ident[:, :], 0.0, 1.0, ALU.mult, ALU.add).then_inc(s_const, 1)
                pool.wait_ge(s_const, 4)
                nc.gpsimd.affine_select(out=pick[:], in_=pick[:], compare_op=ALU.not_equal, fill=1.0,
                                        base=0, pattern=[[0, 1]], channel_multiplier=1).then_inc(s_const, 1)
                pool.wait_ge(s_const, 5)
                nc.gpsimd.memset(two[:], 0.0).then_inc(s_two, 1)
                for half in range(2):
                    pool.wait_ge(s_two, half + 1)
                    nc.gpsimd.affine_select(out=two[:], in_=two[:], compare_op=ALU.not_equal, fill=1.0,
                                            base=-D * half, pattern=[[-1, D]], channel_multiplier=1).then_inc(s_two, 1)
                pool.wait_ge(s_two, 3)
                make_not_diag(nc, pool, v)
                with pool.Fori(0, GROUPS) as grp:
                    pool.wait_ge(s_var, grp + 1)
                    nc.gpsimd.tensor_tensor(out=lsum[:, 3, :], in0=lsum[:, 2, :], in1=power[:, 0:LNG],
                                            op=ALU.pow).then_inc(s_rstd, 1)

            @block.scalar
            def _(act):
                act.dma_start(wstage[0:D, 0, :], v["w_gat"]).then_inc(s_w, 16)
                for dup in range(2):
                    for m in range(2):
                        act.dma_start(wstage[0:D, 2 + 6 * m + dup:2 + 6 * m + 6:2, :],
                                      v["w_ih_e"].rearrange(gate_view, t=3)[:, :, D * m:D * m + D]).then_inc(s_w, 16)
                act.dma_start(wstage[0:D, 14:20:2, :], v["w_hh_e"].rearrange(gate_view, t=3)).then_inc(s_w, 16)
                act.dma_start(wstage[0:D, 15:20:2, :], v["w_hh_n"].rearrange(gate_view, t=3)).then_inc(s_w, 16)
                act.dma_start(wstage[0:D, 20:23, :], v["w_ih_n"].rearrange(gate_view, t=3)).then_inc(s_w, 16)
                with nc.allow_non_contiguous_dma(reason="a few hundred floats, once"):
                    act.dma_start(a12[:, :], v["a_gat"].rearrange("(m d) o -> d (m o)", m=2)).then_inc(s_w, 16)
                    for half, (ih, hh) in enumerate(((v["b_ih_e"], v["b_hh_e"]), (v["b_ih_n"], v["b_hh_n"]))):
                        for which, b in enumerate((ih, hh)):
                            act.dma_start(bias[D * half:D * half + D, which, :],
                                          b.rearrange("(t n) -> n t", t=3)).then_inc(s_w, 16)
                for q in range(XG):
                    act.wait_ge(s_xt, q + 1)
                    nc.scalar.copy(blocks(high2, 4 * q), banked(q % 4)).then_inc(s_hi, 1)
                act.wait_ge(s_wt, 1)
                nc.scalar.copy(wT[:, 0, :], ps[0:D, 1, 0, 0:D]).then_inc(s_wk, 1)
                nc.scalar.copy(wT[:, 1, :], ps[0:D, 1, 0, 0:D]).then_inc(s_wk, 1)
                nc.scalar.copy(wie[:, :, :, :].rearrange("p m t d -> p (m t d)"),
                               ps[:, 1, 1, 0:6 * D]).then_inc(s_wk, 1)
                nc.scalar.copy(whh[:, :, :].rearrange("p t (e d) -> p (t e) d", e=2),
                               ps[0:D, 1, 2, 0:6 * D].rearrange("p (t d) -> p t d", d=D)).then_inc(s_wk, 1)
                nc.scalar.copy(wihn[:, :, :], ps[0:D, 1, 0, D:4 * D].rearrange("p (t d) -> p t d", d=D)
                               ).then_inc(s_wk, 1)
                act.wait_ge(s_wp, 1)
                nc.scalar.copy(va[:, 0, :], ps[:, 1, 3, 0:2]).then_inc(s_wk, 1)
                nc.scalar.copy(va[:, 1, 0:1], ps[:, 1, 3, 1:2]).then_inc(s_wk, 1)
                nc.scalar.copy(va[:, 1, 1:2], ps[:, 1, 3, 0:1]).then_inc(s_wk, 1)
                nc.scalar.copy(w2[D:P, :, :], ps[D:P, 1, 3, D:4 * D].rearrange("p (t d) -> p t d", d=D)
                               ).then_inc(s_wk, 1)
                act.wait_ge(s_wk, 9)
                w_edge, w_node = v["w_edge"], v["w_node"]
                nc.scalar.copy(w_edge[0:D, :, :], wie[0:D, 0, 0:2, :]).then_inc(s_wk, 1)
                nc.scalar.copy(w_edge[D:P, :, :], whh[:, 0:2, 0:D]).then_inc(s_wk, 1)
                nc.scalar.copy(w_node[0:D, :, :], whh[:, 0:2, D:2 * D]).then_inc(s_wk, 1)
                nc.scalar.copy(w_node[D:P, :, :], w2[D:P, 0:2, :]).then_inc(s_wk, 1)

                def split_h(grp):
                    at = bass.ds(grp * LNG, LNG)
                    act.wait_ge(s_ln, grp + 1)
                    nc.scalar.copy(parts[:, at, 0, :], h[:, at, 1:]).then_inc(s_h0, 1)
                    for g in range(G):
                        act.dma_start(scratch[:, bass.ds(grp * LNG + C * g, LNG), :],
                                      h[Q * g:Q * g + Q, at, :]).then_inc(s_scr, 16)

                def make_pair(tile, t):
                    act.wait_ge(s_pair_free, tile + 1)
                    cols = bass.ds(tile * Q, Q)
                    for part, src in ((0, high2), (1, low2)):
                        half = slice(D * part, D * part + D)
                        nc.scalar.copy(pair[half, t % 2, :].rearrange("p (g q) -> p g q", g=G),
                                       src[half, :].bitcast(F32).rearrange("p (g m) -> p g m", g=G)[:, :, cols]
                                       ).then_inc(s_pair, 1)

                assert TPB % 2 == 0
                act.wait_ge(s_hi, XG)
                act.wait_ge(s_low, XG)
                with act.Fori(0, GROUPS) as grp:
                    with act.Fori(0, BODIES) as body:
                        for slot in range(RING):
                            if slot % SPT == 0:
                                make_pair(grp * LNG + body * TPB + slot // SPT, slot // SPT)
                            act.wait_ge(s_strip[slot], (grp * BODIES + body + 1) * (16 * G))
                            act.wait_ge(s_sign_free, grp * (BODIES * RING) + body * RING + slot + 1)
                            unit = grp * (LNG * SPT) + body * RING + slot
                            nc.scalar.activation(
                                signs[:, :], ring[:, slot, :], ACT.Sign,
                                accum_out=rowsign[:, :, :].rearrange("p c s -> p (c s)")[:, bass.ds(unit, 1)]
                            ).then_inc(s_sign, 1)
                            act.wait_ge(s_sign, grp * (BODIES * RING) + body * RING + slot + 1)
                            act.sem_inc(s_sign_free, 1)
                    split_h(grp)

            @block.tensor
            def _(pe):
                pe.wait_ge(s_id, 2)
                for q in range(XG):
                    if q % (XG // 4) == 0:
                        pe.wait_ge(s_x[q // (XG // 4)], 16 * G)
                    if q >= 4:
                        pe.wait_ge(s_low, q - 3)
                    for b in range(4):
                        for half in range(2):
                            last = nc.tensor.matmul(ps[D * half:D * half + D, 0, q % 4, P * b:P * b + P],
                                                    h[:, 4 * q + b, 1:], ident[:], start=True, stop=True,
                                                    skip_group_check=True)
                    last.then_inc(s_xt, 1)
                pe.wait_ge(s_w, 16 * 13)
                id64 = ident[0:D, 0:D]
                nc.tensor.transpose(ps[0:D, 1, 0, 0:D], wstage[0:D, 0, :], id64)
                for t in range(3):
                    nc.tensor.transpose(ps[0:D, 1, 0, D * (t + 1):D * (t + 2)], wstage[0:D, 20 + t, :], id64)
                for m in range(2):
                    for t in range(3):
                        o = 3 * m + t
                        nc.tensor.transpose(ps[:, 1, 1, D * o:D * o + D],
                                            wstage[0:D, 2 + 2 * o:4 + 2 * o, :].rearrange("p a d -> p (a d)"), id64)
                for o in range(6):
                    last = nc.tensor.transpose(ps[0:D, 1, 2, D * o:D * o + D], wstage[0:D, 14 + o, :], id64)
                last.then_inc(s_wt, 1)
                pe.wait_ge(s_wk, 5)
                nc.tensor.matmul(ps[:, 1, 3, 0:2], wT[:, :, :].rearrange("p a d -> p (a d)"), a12[:, :],
                                 start=True, stop=True)
                nc.tensor.matmul(ps[D:P, 1, 3, D:4 * D], wT[:, 0, :], wihn[:, :, :].rearrange("p t d -> p (t d)"),
                                 start=True, stop=True, skip_group_check=True).then_inc(s_wp, 1)
                pe.sem_inc(s_pair_free, 2)
                pe.wait_ge(s_low, XG)
                with pe.Fori(0, C // TPB) as body:
                    for t in range(TPB):
                        pe.wait_ge(s_pair, (body * TPB + t) * 2 + 2)
                        for s in range(SPT):
                            strip = t * SPT + s
                            pe.wait_ge(s_gram_free, body * RING + strip + 1)
                            if strip == 1:
                                pe.wait_ge(s_wk, 13)
                            for b in range(4):
                                cols = slice(STRIP * s + BANK * b, STRIP * s + BANK * (b + 1))
                                o = ps[:, strip % 2, b, :]
                                nc.tensor.matmul(o, pair[:, t % 2, :], high2[:, cols], start=True, stop=False)
                                last = nc.tensor.matmul(o, pair[:, t % 2, :], low2[:, cols], start=False, stop=True)
                            last.then_inc(s_gram, 1)
                        pe.wait_ge(s_gram, body * RING + (t + 1) * SPT)
                        pe.sem_inc(s_pair_free, 1)

            @block.vector
            def _(dve):
                dve.sem_inc(s_gram_free, 2)
                dve.sem_inc(s_sign_free, 1)
                with dve.Fori(0, XG // 4) as four:
                    for i in range(4):
                        dve.wait_ge(s_hi, four * 4 + (i + 1))
                        nc.vector.tensor_tensor(out=blocks(low2, four * 16 + 4 * i), in0=banked(i),
                                                in1=blocks(high2, four * 16 + 4 * i).bitcast(F32),
                                                op=ALU.subtract).then_inc(s_low, 1)
                dve.wait_ge(s_w, 16 * 13)
                nc.vector.tensor_tensor(out=brz[:, :], in0=bias[:, 0, 0:2], in1=bias[:, 1, 0:2],
                                        op=ALU.add).then_inc(s_bias, 1)
                nc.vector.tensor_scalar(out=bhn[:, :], in0=bias[:, 1, 2:3], scalar1=0.5, scalar2=None,
                                        op0=ALU.mult).then_inc(s_bias, 1)
                dve.wait_ge(s_bias, 2)
                nc.vector.tensor_scalar(out=brz[:, :], in0=brz[:, :], scalar1=0.5, scalar2=None,
                                        op0=ALU.mult).then_inc(s_bias, 1)

                LN_STEPS = 8

                def norm(grp):
                    chain = Chain(dve, s_c, grp * LN_STEPS)
                    at = bass.ds(grp * LNG, LNG)
                    hg, wide = h[:, at, 1:], [P, LNG, D]
                    dve.wait_ge(s_gram_free, 2 + (grp + 1) * (LNG * SPT))
                    row_sum = lsum[:, 0, :]
                    chain.after(nc.vector.tensor_reduce(row_sum, outer[:, at, :], AX, ALU.add))
                    dve.wait_ge(s_sign, (grp + 1) * (LNG * SPT))
                    chain.after(nc.vector.tensor_reduce(h[:, at, 0], rowsign[:, at, :], AX, ALU.add))
                    chain.after(nc.vector.tensor_scalar(lsum[:, 1, :], row_sum, -R_CONST, F_CONST, ALU.mult, ALU.add))
                    chain.after(nc.vector.scalar_tensor_tensor(
                        out=sq[:, :, :], in0=hg, scalar=1.0 - B_CONST, in1=lsum[:, 1, :].unsqueeze(2).to_broadcast(wide),
                        op0=ALU.mult, op1=ALU.add))
                    chain.after(nc.vector.tensor_reduce(row_sum, sq[:, :, :], AX, ALU.add))
                    chain.after(nc.vector.tensor_scalar(lsum[:, 1, :], row_sum, 1.0 / D, None, ALU.mult))
                    chain.after(nc.vector.tensor_tensor(
                        out=hg, in0=sq[:, :, :], in1=lsum[:, 1, :].unsqueeze(2).to_broadcast(wide), op=ALU.subtract))
                    chain.after(nc.vector.tensor_tensor(out=sq[:, :, :], in0=hg, in1=hg, op=ALU.mult))
                    assert chain.n == LN_STEPS
                    nc.vector.tensor_reduce(row_sum, sq[:, :, :], AX, ALU.add).then_inc(s_sqsum, 1)
                    dve.wait_ge(s_sqsum, grp + 1)
                    nc.vector.tensor_scalar(lsum[:, 2, :], row_sum, 1.0 / D, EPS, ALU.mult, ALU.add).then_inc(s_var, 1)
                    dve.wait_ge(s_rstd, grp + 1)
                    nc.vector.tensor_tensor(out=hg, in0=hg, in1=lsum[:, 3, :].unsqueeze(2).to_broadcast(wide),
                                            op=ALU.mult).then_inc(s_ln, 1)
                    dve.wait_ge(s_h0, grp + 1)
                    nc.vector.tensor_tensor(out=parts[:, at, 1, :], in0=hg, in1=parts[:, at, 0, :].bitcast(F32),
                                            op=ALU.subtract).then_inc(s_h1, 1)

                flat = outer[:, :, :].rearrange("p c s -> p (c s)")
                with dve.Fori(0, GROUPS) as grp:
                    with dve.Fori(0, BODIES) as body:
                        for slot in range(RING):
                            unit = grp * (LNG * SPT) + body * RING + slot
                            dve.wait_ge(s_strip[slot], (grp * BODIES + body + 1) * (16 * G))
                            dve.wait_ge(s_gram, unit + 1)
                            dve.wait_ge(s_gram_free, unit + 2)
                            nc.vector.scalar_tensor_tensor(
                                out=weighed[:, :], in0=ring[:, slot, :], scalar=1.0,
                                in1=ps[:, slot % 2, :, :].rearrange("p b n -> p (b n)"), op0=ALU.mult, op1=ALU.mult,
                                accum_out=flat[:, bass.ds(unit, 1)]).then_inc(s_gram_free, 1)
                    norm(grp)
                dve.wait_ge(s_h1, GROUPS)


def layer1(nc, v):
    K, flag = v["K"], v["flag"]
    with ExitStack() as ctx:
        def sb(name, shape, dt):
            return ctx.enter_context(nc.sbuf_tensor(name, shape, dt))

        b = dict(v)
        b["at"] = sb("at", [P, 4, v["HC"], BANK], F32)
        b["mask"] = sb("mask", [P, 2, v["HC"], BANK], F32R)
        b["nat"] = sb("nat", [P, 4, D], F32)
        b["stage"] = sb("stage", [P, 4, 1 + D], F32)
        b["hT"] = sb("hT", [P, BANK], F32)
        b["sums"] = sb("sums", [P, 2, BANK], F32)
        b["wsum"] = sb("wsum", [P, 2, BANK], F32)
        b["tr"] = sb("tr", [P, BANK], F32)
        b["tz"] = sb("tz", [P, BANK], F32)
        b["hn"] = sb("hn", [P, BANK], F32)
        b["nn"] = sb("nn", [P, BANK], F32)
        b["en"] = sb("en", [P, 4, 4], F32)
        b["co"] = sb("co", [P, 8, 4, 3], F32)
        b["prob"] = sb("prob", [P, 2, 4, D], F32)
        b["cnt"] = [b["tr"], b["tz"]]
        b["lows"] = b["nn"]
        b["seen"] = sb("seen", [P, K * v["H"]], F32)
        b["seen_k"] = sb("seen_k", [P, K], F32)
        b["pcount"] = sb("pcount", [P, K, 4], F32)
        b["dsign"] = sb("dsign", [P, K, 4], F32)
        b["seen4"] = sb("seen4", [P, K], F32)
        b["miss"] = sb("miss", [1, K + 1], F32)
        b["y"] = sb("y", [P, 4, D], F32)
        b["ysq"] = sb("ysq", [P, 4, D], F32)
        b["yo"] = sb("yo", [P, 4, D], F32)
        b["ls"] = sb("ls", [P, 4, 4], F32)
        b["s_dsign"] = v["sem"]("diagonal_signs")
        b["ps"] = ctx.enter_context(nc.psum_tensor("ps1", [P, 8, BANK], F32))
        fast = Sweep(nc, b, "f_", 1)
        full = Sweep(nc, b, "g_", 2)
        b["s_miss"], b["s_missed"], b["s_flag"] = v["sem"]("misses_by_row"), v["sem"]("misses"), v["sem"]("flag_made")
        with nc.Block() as block:
            @block.sync
            def _(sp):
                fast.sync(sp)

            @block.gpsimd
            def _(pool):
                fast.gpsimd(pool)

            @block.scalar
            def _(act):
                fast.scalar(act)

            @block.tensor
            def _(pe):
                fast.tensor(pe)
                pe.wait_ge(b["s_miss"], 4)
                nc.tensor.matmul(b["ps"][0:1, HN, 0:K], b["one"][:, :], b["seen_k"][:, :], start=True,
                                 stop=True).then_inc(b["s_missed"], 1)

            @block.vector
            def _(dve):
                fast.vector(dve)
                compare(nc, dve, b, fast)

        with nc.Block() as block:
            @block.sync
            def _(sp):
                with sp.If(sp.value_load(flag[0:1, 0:1], min_val=0, max_val=1) > 0):
                    full.sync(sp)

            @block.gpsimd
            def _(pool):
                with pool.If(pool.value_load(flag[0:1, 0:1], min_val=0, max_val=1) > 0):
                    full.gpsimd(pool)

            @block.scalar
            def _(act):
                with act.If(act.value_load(flag[0:1, 0:1], min_val=0, max_val=1) > 0):
                    full.scalar(act)

            @block.tensor
            def _(pe):
                with pe.If(pe.value_load(flag[0:1, 0:1], min_val=0, max_val=1) > 0):
                    full.tensor(pe)

            @block.vector
            def _(dve):
                with dve.If(dve.value_load(flag[0:1, 0:1], min_val=0, max_val=1) > 0):
                    full.vector(dve)


def compare(nc, dve, b, fast):
    K, s_miss = b["K"], b["s_miss"]
    assert BANK * b["N"] < 1 << 24
    dve.wait_ge(fast.s["mask_ready"], K * b["H"])
    nc.vector.tensor_reduce(b["seen_k"][:, :], b["seen"][:, :].rearrange("p (k h) -> p k h", k=K), AX,
                            ALU.add).then_inc(s_miss, 1)
    nc.vector.tensor_reduce(b["seen4"][:, :], b["pcount"][:, :, :], AX, ALU.add).then_inc(s_miss, 1)
    dve.wait_ge(s_miss, 2)
    nc.vector.tensor_tensor(out=b["seen_k"][:, :], in0=b["seen_k"][:, :], in1=b["seen4"][:, :],
                            op=ALU.subtract).then_inc(s_miss, 1)
    dve.wait_ge(s_miss, 3)
    dve.sem_inc(s_miss, 1)
    dve.wait_ge(b["s_missed"], 1)
    nc.vector.tensor_scalar(b["miss"][:, 0:K], b["ps"][0:1, HN, 0:K], 0.0, None, ALU.not_equal).then_inc(s_miss, 1)
    dve.wait_ge(s_miss, 5)
    nc.vector.tensor_reduce(b["miss"][:, K:K + 1], b["miss"][:, 0:K], AX, ALU.max).then_inc(s_miss, 1)
    dve.wait_ge(s_miss, 6)
    nc.vector.tensor_copy(b["flag"][:, :], b["miss"][:, K:K + 1]).then_inc(b["s_flag"], 1)
    dve.wait_ge(b["s_flag"], 1)


def make_not_diag(nc, pool, b):
    U = b["U"] // 2
    nc.gpsimd.memset(b["not_diag"][:], 1.0).then_inc(b["s_nd"], 1)
    for g in range(G):
        pool.wait_ge(b["s_nd"], g + 1)
        nd = b["not_diag"][Q * g:Q * g + Q, bass.DynSlice(g * U * U, U, step=U + 1), :]
        nc.gpsimd.affine_select(out=nd, in_=nd, compare_op=ALU.not_equal, fill=0.0, base=0,
                                pattern=[[0, U], [-1, Q]], channel_multiplier=1).then_inc(b["s_nd"], 1)
    pool.wait_ge(b["s_nd"], G + 1)


ACC_T, ACC_S, ACC_C = 0, 1, 2
R, Z, IN, HN, MISC = 3, 4, 5, 6, 7


class Sweep:

    SEMS = (
        "diagonal_out turned split_ready mask_ready weighed_done added_done weighed_low_copied "
        "added_low_copied count_copied added_copied weighed_copied summed counts by_row_ready "
        "probabilities_ready exps_ready logits_ready probabilities_spread scaled ht_turned ht_ready "
        "gates tanh_r_ready tanh_z_ready h_part_ready new_input_ready new_ready state_ready "
        "turned_back y_read variance_ready rstd_ready result_ready stored rows_loaded rows_used "
        "staged_loaded chain")

    def __init__(self, nc, b, prefix, signs):
        self.nc, self.b, self.signs, self.prefix = nc, b, signs, prefix
        self.s = {n: b["sem"](prefix + n) for n in self.SEMS.split()}
        self.N, self.K, self.U, self.H = b["N"], b["K"], b["U"], b["H"]
        self.GQ = b["GQ"]

    def where(self, position):
        return min(position, self.H)

    def products_done(self, k):
        return (k + 1) * (self.H * self.signs) + (self.signs - 1)

    def sync(self, sp):
        b, s, U, prefix = self.b, self.s, self.U, self.prefix
        slots = b["SLOTS"]
        for u in range(U):
            if u >= slots:
                sp.wait_ge(s["turned"], 2 * (u + 1 - slots))
            if self.signs == 2 or u >= slots:
                load_unit(sp, b, prefix, 0, u)
        with sp.Fori(1, self.K) as k:
            for u in range(U):
                sp.wait_ge(s["turned"], k * (2 * U) + 2 * (u + 1 - slots))
                load_unit(sp, b, prefix, k, u)

    def gpsimd(self, pool):
        nc, b, s = self.nc, self.b, self.s
        U, RB, UC, K, SLOTS = self.U, b["RB"], b["UC"], self.K, b["SLOTS"]

        def no_diagonal(k):
            for u in range(U):
                raw = unit_view(b, u % SLOTS)[:, (u % 2) * UC * (UC * Q):(u % 2 + 1) * UC * (UC * Q)]
                diag = bass.AP(tensor=raw.tensor, offset=raw.offset,
                               ap=[list(raw.ap[0]), [UC * Q + Q, UC], [1, Q]])
                pool.wait_ge(b["s_raw"][self.prefix][u % SLOTS], (k * (U // SLOTS) + u // SLOTS + 1) * (16 * G))
                carry(pool, b["s_carry"])
                nc.gpsimd.tensor_tensor(
                    out=diag, in0=diag,
                    in1=b["not_diag"][:, bass.ds(k * (U // 2) + u // 2, 1), :].to_broadcast([P, UC, Q]),
                    op=ALU.mult).then_inc(s["diagonal_out"], 1)

        def end(k):
            pool.wait_ge(s["variance_ready"], k + 1)
            nc.gpsimd.tensor_tensor(out=b["ls"][:, 3, :], in0=b["ls"][:, 2, :], in1=b["power"][:, 0:4],
                                    op=ALU.pow).then_inc(s["rstd_ready"], 1)

        if self.signs == 2:
            with pool.Fori(0, K) as k:
                no_diagonal(k)
                end(k)
        else:
            no_diagonal(0)
            with pool.Fori(1, K) as k:
                no_diagonal(k)
                end(k - 1)
            end(K - 1)

    def vector(self, dve):
        nc, b, s, ps = self.nc, self.b, self.s, self.b["ps"]
        H, HC, RB, UC, K, N, signs = self.H, b["HC"], b["RB"], b["UC"], self.K, self.N, self.signs
        hi = slice(D, P)

        def turn(k, half, first):
            n = k * H + half
            u, part = half // 2, half % 2
            if part == 0:
                dve.wait_ge(s["diagonal_out"], k * self.U + u + 1)
            slot = half % 4 if signs == 1 else 0
            if signs == 1:
                if not (first and half < 4):
                    dve.wait_ge(s["weighed_done"], n - 3)
                    dve.wait_ge(s["mask_ready"], n - 3)
            raw = unit_view(b, u % b["SLOTS"]).rearrange("p (f c q) -> p f c q", f=RB, q=Q)
            nc.vector.transpose(
                b["at"][:, slot, :, :].rearrange("p c (f q) -> p f c q", q=Q),
                raw[:, :, HC * part:HC * part + HC, :]).then_inc(s["turned"], 1)
            if signs == 2:
                dve.wait_ge(s["turned"], n + 1)
                for i, sign in enumerate((1.0, -1.0)):
                    m = n * 2 + i
                    dve.wait_ge(s["added_done"], m + 1)
                    dve.wait_ge(s["weighed_done"], m + 1)
                    nc.vector.tensor_scalar(b["at"][:, 1, :, :], b["at"][:, 0, :, :], sign, 0.0,
                                            ALU.mult, ALU.max).then_inc(s["split_ready"], 1)
                    nc.vector.tensor_scalar(b["mask"][:, 0, :, :], b["at"][:, 0, :, :], sign, 0.0,
                                            ALU.mult, ALU.is_gt).then_inc(s["mask_ready"], 1)
                    dve.wait_ge(s["split_ready"], m + 1)
                    dve.wait_ge(s["mask_ready"], m + 1)

        CHAIN = {1: 23, 2: 32}[signs]

        def evac(k, c):
            dve.wait_ge(s["added_done"], self.products_done(k))
            for i in range(signs):
                wsum, sums = b["wsum"][hi, i, :], b["sums"][0:D, i, :]
                nc.vector.tensor_copy(wsum, ps[hi, 3 * i + ACC_T, :]).then_inc(s["weighed_copied"], 1)
                nc.vector.tensor_copy(sums, ps[0:D, 3 * i + ACC_S, :]).then_inc(s["added_copied"], 1)
                dve.wait_ge(s["weighed_copied"], k * signs + i + 1)
                dve.wait_ge(s["weighed_low_copied"], k * signs + i + 1)
                c.after(nc.vector.tensor_tensor(out=wsum, in0=wsum, in1=b["lows"][hi, :], op=ALU.add))
                dve.wait_ge(s["added_copied"], k * signs + i + 1)
                dve.wait_ge(s["added_low_copied"], k * signs + i + 1)
                nc.vector.tensor_tensor(out=sums, in0=sums, in1=b["lows"][0:D, :], op=ALU.add).then_inc(s["summed"], 1)

        def counts(k, c):
            dve.wait_ge(s["staged_loaded"], (k + 1) * (16 * G))
            carry(dve, b["s_carry"])
            nc.vector.tensor_tensor(out=b["pcount"][:, bass.ds(k, 1), :].rearrange("p k e -> p (k e)"),
                                    in0=b["stage"][:, :, 0],
                                    in1=b["dsign"][:, bass.ds(k, 1), :].rearrange("p k e -> p (k e)"),
                                    op=ALU.subtract).then_inc(s["counts"], 1)
            dve.wait_ge(s["counts"], k + 2)

        def softmax(k, c):
            en, co = b["en"], b["co"]
            logit, count = en[:, :, 0:signs], en[:, :, 2:2 + signs]
            if signs == 1:
                count = b["pcount"][:, bass.ds(k, 1), :].rearrange("p k e -> p (k e)").unsqueeze(2)
            col = lambda j, w=signs: co[:, j, :, 0:w]
            dve.wait_ge(s["by_row_ready"], k + 1)
            for part in (0, 2)[0:signs]:
                c.after(nc.vector.tensor_copy(
                    en[:, :, part:part + signs],
                    ps[:, HN, 0:16].rearrange("p (b e) -> p b e", b=4)[:, :, part:part + signs]))
            c.after(nc.vector.scalar_tensor_tensor(out=col(0), in0=logit, scalar=ALPHA, in1=logit,
                                                   op0=ALU.mult, op1=ALU.max))
            c.after(nc.vector.tensor_scalar(col(1), count, 0.0, None, ALU.is_gt))
            c.after(nc.vector.tensor_tensor(out=col(0), in0=col(0), in1=col(1), op=ALU.mult))
            c.after(nc.vector.tensor_scalar(col(1), col(1), -1.0, -NEG_INF, ALU.add, ALU.mult))
            c.after(nc.vector.tensor_tensor(out=col(0), in0=col(0), in1=col(1), op=ALU.add))
            if signs == 2:
                c.after(nc.vector.tensor_tensor(out=co[:, 2, :, 0], in0=co[:, 0, :, 0], in1=co[:, 0, :, 1],
                                                op=ALU.max))
                c.after(nc.vector.tensor_scalar(co[:, 2, :, 0], co[:, 2, :, 0], NEG_INF, None, ALU.max))
            else:
                c.after(nc.vector.tensor_scalar(co[:, 2, :, 0], co[:, 0, :, 0], NEG_INF, None, ALU.max))
            for i in range(signs):
                c.after(nc.vector.tensor_tensor(out=co[:, 3, :, i], in0=co[:, 0, :, i], in1=co[:, 2, :, 0],
                                                op=ALU.subtract))
            nc.vector.tensor_scalar(co[:, 3, :, signs], co[:, 2, :, 0], -1.0, NEG_INF, ALU.mult,
                                    ALU.add).then_inc(s["logits_ready"], 1)
            if signs == 2:
                c.after(nc.vector.tensor_tensor(out=co[:, 5, :, 0], in0=en[:, :, 2], in1=en[:, :, 3], op=ALU.add))
                c.after(nc.vector.tensor_scalar(co[:, 5, :, 2], co[:, 5, :, 0], -1.0, float(N), ALU.mult, ALU.add))
            else:
                c.after(nc.vector.tensor_scalar(co[:, 5, :, 2:3], count, -1.0, float(N), ALU.mult, ALU.add))

        def probabilities(k, c):
            en, co = b["en"], b["co"]
            zeros = co[:, 5, :, 2]
            count = en[:, :, 2:2 + signs]
            if signs == 1:
                count = b["pcount"][:, bass.ds(k, 1), :].rearrange("p k e -> p (k e)").unsqueeze(2)
            dve.wait_ge(s["exps_ready"], k + 1)
            c.after(nc.vector.tensor_tensor(out=co[:, 6, :, 0:signs], in0=co[:, 4, :, 0:signs], in1=count,
                                            op=ALU.mult))
            c.after(nc.vector.tensor_tensor(out=co[:, 6, :, 2], in0=co[:, 4, :, signs], in1=zeros, op=ALU.mult))
            for i in range(signs):
                c.after(nc.vector.tensor_tensor(out=co[:, 6, :, 2], in0=co[:, 6, :, 2], in1=co[:, 6, :, i],
                                                op=ALU.add))
            c.after(nc.vector.reciprocal(co[:, 7, :, 0], co[:, 6, :, 2]))
            for i in range(signs):
                c.after(nc.vector.tensor_tensor(out=co[:, 7, :, 1 + i], in0=co[:, 4, :, i], in1=co[:, 7, :, 0],
                                                op=ALU.mult))
                nc.vector.tensor_copy(b["prob"][:, i, :, :],
                                      co[:, 7, :, 1 + i:2 + i].to_broadcast([P, 4, D])).then_inc(s["probabilities_ready"], 1)

        def scale(k, c):
            dve.wait_ge(s["probabilities_spread"], k + 1)
            if signs == 2:
                c.after(nc.vector.tensor_tensor(out=b["wsum"][hi, 1, :], in0=ps[hi, R, :], in1=b["wsum"][hi, 1, :],
                                                op=ALU.mult))
                c.after(nc.vector.tensor_tensor(out=b["wsum"][hi, 0, :], in0=ps[hi, IN, :], in1=b["wsum"][hi, 0, :],
                                                op=ALU.mult))
                nc.vector.tensor_tensor(out=b["wsum"][hi, 0, :], in0=b["wsum"][hi, 0, :], in1=b["wsum"][hi, 1, :],
                                        op=ALU.subtract).then_inc(s["scaled"], 1)
            else:
                nc.vector.tensor_tensor(out=b["wsum"][hi, 0, :], in0=ps[hi, IN, :], in1=b["wsum"][hi, 0, :],
                                        op=ALU.mult).then_inc(s["scaled"], 1)

        def reset(k, c):
            dve.wait_ge(s["tanh_r_ready"], k + 1)
            dve.wait_ge(s["h_part_ready"], k + 1)
            dve.wait_ge(s["gates"], k * 3 + 2)
            c.after(nc.vector.scalar_tensor_tensor(out=b["hn"][:, :], in0=b["tr"][:, :], scalar=1.0,
                                                   in1=b["hn"][:, :], op0=ALU.add, op1=ALU.mult))
            nc.vector.tensor_tensor(out=b["hn"][:, :], in0=ps[:, IN, :], in1=b["hn"][:, :],
                                    op=ALU.add).then_inc(s["new_input_ready"], 1)

        def update(k, c):
            dve.wait_ge(s["new_ready"], k + 1)
            dve.wait_ge(s["ht_ready"], (k + 1) * 3)
            dve.wait_ge(s["tanh_z_ready"], k + 1)
            c.after(nc.vector.tensor_tensor(out=b["hT"][:, :], in0=b["hT"][:, :], in1=b["nn"][:, :],
                                            op=ALU.subtract))
            c.after(nc.vector.scalar_tensor_tensor(out=b["tz"][:, :], in0=b["tz"][:, :], scalar=1.0,
                                                   in1=b["hT"][:, :], op0=ALU.add, op1=ALU.mult))
            nc.vector.scalar_tensor_tensor(out=b["hT"][:, :], in0=b["tz"][:, :], scalar=0.5, in1=b["nn"][:, :],
                                           op0=ALU.mult, op1=ALU.add).then_inc(s["state_ready"], 1)

        def norm(k, c):
            y, ls, wide = b["y"], b["ls"], [P, 4, D]
            dve.wait_ge(s["turned_back"], k + 1)
            dve.wait_ge(s["rows_loaded"], (k + 1) * (16 * G))
            nc.vector.tensor_tensor(
                out=y[:, :, :], in0=ps[:, MISC, 0:4 * D].rearrange("p (b d) -> p b d", d=D),
                in1=b["dnat"][:, bass.ds(k * 4, 4)].unsqueeze(2).to_broadcast(wide), op=ALU.mult).then_inc(s["y_read"], 1)
            dve.wait_ge(s["y_read"], k + 2)
            nc.vector.tensor_tensor(out=y[:, :, :], in0=y[:, :, :], in1=b["nat"][:, :, :],
                                    op=ALU.add).then_inc(s["rows_used"], 1)
            dve.wait_ge(s["rows_used"], k + 2)
            c.after(nc.vector.tensor_reduce(ls[:, 0, :], y[:, :, :], AX, ALU.add))
            c.after(nc.vector.tensor_scalar(ls[:, 1, :], ls[:, 0, :], 1.0 / D, None, ALU.mult))
            c.after(nc.vector.tensor_tensor(out=y[:, :, :], in0=y[:, :, :],
                                            in1=ls[:, 1, :].unsqueeze(2).to_broadcast(wide), op=ALU.subtract))
            c.after(nc.vector.tensor_tensor(out=b["ysq"][:, :, :], in0=y[:, :, :], in1=y[:, :, :], op=ALU.mult))
            c.after(nc.vector.tensor_reduce(ls[:, 0, :], b["ysq"][:, :, :], AX, ALU.add))
            nc.vector.tensor_scalar(ls[:, 2, :], ls[:, 0, :], 1.0 / D, EPS, ALU.mult, ALU.add).then_inc(s["variance_ready"], 1)

        def result(k, c):
            dve.wait_ge(s["rstd_ready"], k + 1)
            dve.wait_ge(s["stored"], k * 16 + 16)
            nc.vector.tensor_tensor(out=b["yo"][:, :, :], in0=b["y"][:, :, :],
                                    in1=b["ls"][:, 3, :].unsqueeze(2).to_broadcast([P, 4, D]),
                                    op=ALU.mult).then_inc(s["result_ready"], 1)

        if signs == 1:
            dve.wait_ge(b["s_dsign"], 1)
            dve.sem_inc(s["counts"], 1)
        dve.sem_inc(s["y_read"], 1)
        dve.sem_inc(s["rows_used"], 1)
        dve.sem_inc(s["stored"], 16)
        steps = ((counts, 1), (evac, 2), (softmax, 5), (probabilities, 6), (scale, 8), (reset, 10), (update, 12),
                 (norm, 14), (result, 16))
        if signs == 2:
            steps = steps[1:]
        self.weave(dve, turn, steps, CHAIN)

    def weave(self, eng, half_step, steps, chain_length=None):
        def run(k, first, prev):
            chain = None if prev is None or chain_length is None else Chain(eng, self.s["chain"], prev * chain_length)

            def at(position):
                for step, where in steps:
                    if prev is not None and self.where(where) == position:
                        step(prev, chain)

            for half in range(self.H):
                at(half)
                if k is not None:
                    half_step(k, half, first)
            at(self.H)
            if chain is not None and chain.n != chain_length:
                raise AssertionError(chain.n)

        if self.signs == 2:
            run(0, True, None)
            run(None, False, 0)
            with eng.Fori(1, self.K) as i:
                run(i, False, None)
                run(None, False, i)
        else:
            run(0, True, None)
            with eng.Fori(1, self.K) as i:
                run(i, False, i - 1)
            run(None, False, self.K - 1)

    def scalar(self, act):
        nc, b, s, ps, RB = self.nc, self.b, self.s, self.b["ps"], self.b["RB"]
        H, signs = self.H, self.signs
        hi = slice(D, P)

        def chunk_rows(k, g):
            return b["scratch"][:, bass.ds(k * RB, RB), :].rearrange("j (b m) d -> j b m d", m=G)[:, :, g, :]

        def sign(k, half, first):
            if half == H // 4:
                if first:
                    act.wait_ge(b["s_scr"], 16 * G * (b["C"] // b["LNG"]))
                staged_rows(k, first)
            if signs == 2:
                return
            n = k * H + half
            act.wait_ge(s["turned"], n + 1)
            if not (first and half < 2):
                act.wait_ge(s["added_done"], n - 1)
            nc.scalar.activation(
                b["mask"][:, half % 2, :, :].rearrange("p c i -> p (c i)"),
                b["at"][:, half % 4, :, :].rearrange("p c i -> p (c i)").bitcast(U32), ACT.Sign,
                accum_out=b["seen"][:, bass.ds(n, 1)]).then_inc(s["mask_ready"], 1)

        def evac(k, c):
            act.wait_ge(s["added_done"], self.products_done(k))
            for i in range(signs):
                if i == 1:
                    act.wait_ge(s["summed"], k * signs + 1)
                nc.scalar.copy(b["lows"][hi, :], ps[0:D, 3 * i + ACC_T, :]).then_inc(s["weighed_low_copied"], 1)
                nc.scalar.copy(b["lows"][0:D, :], ps[hi, 3 * i + ACC_S, :]).then_inc(s["added_low_copied"], 1)
                if signs == 2:
                    nc.scalar.copy(b["cnt"][i][0:D, :], ps[0:D, 3 * i + ACC_C, :]).then_inc(s["count_copied"], 1)
            act.wait_ge(s["ht_turned"], k + 1)
            nc.scalar.copy(b["hT"][:, :], ps[:, MISC, :]).then_inc(s["ht_ready"], 1)
            nc.scalar.copy(b["sums"][hi, 0, :], ps[hi, MISC, :]).then_inc(s["ht_ready"], 1)
            nc.scalar.copy(b["wsum"][0:D, 0, :], ps[0:D, MISC, :]).then_inc(s["ht_ready"], 1)

        def exps(k, c):
            act.wait_ge(s["logits_ready"], k + 1)
            nc.scalar.activation(b["co"][:, 4, :, 0:signs + 1], b["co"][:, 3, :, 0:signs + 1],
                                 ACT.Exp).then_inc(s["exps_ready"], 1)

        def gates(k, c):
            act.wait_ge(s["gates"], k * 3 + 1)
            nc.scalar.activation(b["tr"][:, :], ps[:, R, :], ACT.Tanh, bias=b["brz"][:, 0:1],
                                 scale=0.5).then_inc(s["tanh_r_ready"], 1)
            nc.scalar.activation(b["hn"][:, :], ps[:, HN, :], ACT.Identity, bias=b["bhn"][:, 0:1],
                                 scale=0.5).then_inc(s["h_part_ready"], 1)
            act.wait_ge(s["gates"], k * 3 + 3)
            nc.scalar.activation(b["tz"][:, :], ps[:, Z, :], ACT.Tanh, bias=b["brz"][:, 1:2],
                                 scale=0.5).then_inc(s["tanh_z_ready"], 1)

        def new(k, c):
            act.wait_ge(s["new_input_ready"], k + 1)
            nc.scalar.activation(b["nn"][:, :], b["hn"][:, :], ACT.Tanh,
                                 bias=b["bias"][:, 0, 2:3]).then_inc(s["new_ready"], 1)

        def rows(k, c):
            act.wait_ge(s["rows_used"], k + 1)
            for g in range(G):
                act.dma_start(b["nat"][Q * g:Q * g + Q, :, :], chunk_rows(k, g)[:, :, 1:]).then_inc(s["rows_loaded"], 16)

        def staged_rows(k, first):
            if not first:
                act.wait_ge(s["ht_turned"], k)
            if signs == 1:
                act.wait_ge(s["counts"], k + 1)
            for g in range(G):
                act.dma_start(b["stage"][Q * g:Q * g + Q, :, :], chunk_rows(k, g)).then_inc(s["staged_loaded"], 16)

        def store(k, c):
            act.wait_ge(s["result_ready"], k + 1)
            act.dma_start(b["out"][bass.ds(k * BANK, BANK), :].rearrange("(b p) d -> p b d", p=P),
                          b["yo"][:, :, :]).then_inc(s["stored"], 16)

        if signs == 1:
            nc.scalar.activation(b["dsign"][:, :, :].rearrange("p k e -> p (k e)"), b["dnat"][:, :],
                                 ACT.Sign).then_inc(b["s_dsign"], 1)
        self.weave(act, sign, ((rows, 1), (evac, 1), (exps, 5), (gates, 8), (new, 10), (store, 16)))
        act.wait_ge(s["stored"], 16 * (self.K + 1))

    def tensor(self, pe):
        nc, b, s, ps = self.nc, self.b, self.s, self.b["ps"]
        H, HC, signs = self.H, b["HC"], self.signs
        hi = slice(D, P)
        h, parts = b["h"], b["parts"][:, :, :, :].rearrange("p c e d -> p c (e d)")
        mm = nc.tensor.matmul

        def products(k, half, first):
            for i in range(signs):
                n = (k * H + half) * signs + i
                slot = half % 4 if signs == 1 else 1
                mslot = half % 2 if signs == 1 else 0
                if half == 0 and i == 0 and not first:
                    pe.wait_ge(s["weighed_low_copied"], k * signs)
                    pe.wait_ge(s["weighed_copied"], k * signs)
                pe.wait_ge(s["turned" if signs == 1 else "split_ready"], n + 1)
                for cl in range(HC):
                    c = half * HC + cl
                    o = ps[D * (cl % 2):D * (cl % 2) + D, 3 * i + ACC_T, :]
                    last = mm(o, h[:, c, 1:], b["at"][:, slot, cl, :], start=c < 2, stop=c >= H * HC - 2)
                last.then_inc(s["weighed_done"], 1)
                if half == 0 and i == 0 and not first:
                    pe.wait_ge(s["added_low_copied"], k * signs)
                    pe.wait_ge(s["added_copied"], k * signs)
                    if signs == 2:
                        pe.wait_ge(s["count_copied"], k * signs)
                pe.wait_ge(s["mask_ready"], n + 1)
                for cl in range(HC):
                    c = half * HC + cl
                    ends = dict(start=c == 0, stop=c == H * HC - 1)
                    last = mm(ps[:, 3 * i + ACC_S, :], parts[:, c, :], b["mask"][:, mslot, cl, :], **ends)
                    if signs == 2:
                        last = mm(ps[:, 3 * i + ACC_C, :], b["ones"][:, :], b["mask"][:, mslot, cl, :], **ends)
                last.then_inc(s["added_done"], 1)

        def turn_h(k, c):
            pe.wait_ge(s["staged_loaded"], (k + 1) * (16 * G))
            pe.wait_ge(s["y_read"], k + 1)
            for i in range(4):
                for half in range(2):
                    last = mm(ps[D * half:D * half + D, MISC, P * i:P * i + P], b["stage"][:, i, 1:], b["ident"][:],
                              start=True, stop=True)
            last.then_inc(s["ht_turned"], 1)

        def small(k, c):
            pe.wait_ge(s["summed"], (k + 1) * signs)
            if signs == 2:
                pe.wait_ge(s["count_copied"], (k + 1) * signs)
            en = ps[:, HN, 0:16].rearrange("p (b e) -> p b e", b=4)
            for q in range(4):
                cols = slice(P * q, P * q + P)
                for i in range(signs):
                    last = mm(en[:, q, 0:signs], b["sums"][0:D, i, cols], b["va"][0:D, i, 0:signs],
                       start=i == 0, stop=i == signs - 1)
                if signs == 2:
                    for i in range(signs):
                        last = mm(en[:, q, 2 + i:3 + i], b["cnt"][i][0:D, cols], b["pick"][0:D, :], start=True, stop=True)
            last.then_inc(s["by_row_ready"], 1)

        def spread(k, c):
            pe.wait_ge(s["probabilities_ready"], (k + 1) * signs)
            for i in range(signs):
                for q in range(4):
                    last = mm(ps[hi, (IN, R)[i], P * q:P * q + P], b["prob"][:, i, q, :], b["ident"][:, :],
                              start=True, stop=True)
            last.then_inc(s["probabilities_spread"], 1)

        def gates(k, c):
            pe.wait_ge(s["ht_ready"], (k + 1) * 3)
            sums, wsum, lo = b["sums"], b["wsum"], slice(0, D)
            mm(ps[:, HN, :], b["whh"][:, 2, :], b["hT"][0:D, :], start=True, stop=True)
            pe.wait_ge(s["scaled"], k + 1)

            def r_or_z(t, bank):
                mm(ps[lo, bank, :], b["w_edge"][:, t, :], sums[:, 0, :], start=True, stop=signs == 1)
                if signs == 2:
                    mm(ps[lo, bank, :], b["wie"][lo, 1, t, :], sums[lo, 1, :], start=False, stop=True)
                mm(ps[hi, bank, :], b["w_node"][:, t, :], wsum[:, 0, :], start=True, stop=True,
                   skip_group_check=True).then_inc(s["gates"], 1)

            r_or_z(0, R)
            for i in range(signs):
                mm(ps[lo, IN, :], b["wie"][lo, i, 2, :], sums[lo, i, :], start=i == 0, stop=i == signs - 1)
            mm(ps[hi, IN, :], b["w2"][hi, 2, :], wsum[hi, 0, :], start=True, stop=True,
               skip_group_check=True).then_inc(s["gates"], 1)
            r_or_z(1, Z)

        def back(k, c):
            pe.wait_ge(s["state_ready"], k + 1)
            for q in range(4):
                last = mm(ps[:, MISC, D * q:D * q + D], b["hT"][:, P * q:P * q + P], b["two"][:, :],
                          start=True, stop=True)
            last.then_inc(s["turned_back"], 1)

        if signs == 2:
            pe.sem_inc(s["weighed_done"], 1)
            pe.sem_inc(s["added_done"], 1)
        self.weave(pe, products, ((turn_h, 0), (small, 2), (spread, 5), (gates, 7), (back, 11)))


_INS = ["x", "adj", "L1_gnn_W_gat", "L1_gnn_a_gat", "L1_gnn_w_ih_e", "L1_gnn_w_hh_e", "L1_gnn_b_ih_e",
        "L1_gnn_b_hh_e", "L1_gnn_w_ih_n", "L1_gnn_w_hh_n", "L1_gnn_b_ih_n", "L1_gnn_b_hh_n"]


def kernel(**inputs):
    import numpy as _np
    import concourse.bacc as _bacc
    from concourse import mybir as _mybir
    from concourse.bass_utils import run_bass_kernel_spmd as _run

    nc = _bacc.Bacc("TRN2", target_bir_lowering=False, num_devices=1)
    arrays, args = {}, []
    for name in _INS:
        a = _np.ascontiguousarray(inputs[name])
        arrays[f"in_{name}"] = a
        args.append(nc.dram_tensor(f"in_{name}", a.shape, _mybir.dt.from_np(a.dtype), kind="ExternalInput").ap())
    shape = inputs["x"].shape
    out = nc.dram_tensor("out_0", shape, _mybir.dt.float32, kind="ExternalOutput").ap()
    build_gnn(nc, *args, out)
    return _run(nc, [arrays], core_ids=[0]).results[0]["out_0"]
```
